# Optimizing a Trainium2 kernel written in Bass

```python
import numpy as np
import jax
import jax.numpy as jnp

def _softmax(x, axis=-1):
    return jax.nn.softmax(x, axis=axis)

def _gelu(x):
    return jax.nn.gelu(x, approximate=True)

def _silu(x):
    return jax.nn.silu(x)

def _sigmoid(x):
    return jax.nn.sigmoid(x)

def _layernorm(x, axis=-1, eps=1e-05):
    m = jnp.mean(x, axis=axis, keepdims=True)
    v = jnp.var(x, axis=axis, keepdims=True)
    return (x - m) / jnp.sqrt(v + eps)

def _scatter_add(tgt, idx, src, axis=0):
    return tgt.at[idx].add(src)

def _segment_sum(src, seg, n):
    return jax.ops.segment_sum(src, seg, n)
kernel_name = 'mk_adaln_d1_jaxref_r8_b32f40'

def setup_inputs(seed: int=0):
    np.random.seed(seed)
    _w = jnp.asarray

    def _L0_attn_setup():
        import jax, jax.numpy as jnp
        import numpy as np
        EMB_DIM = 33
        FREQ = 10.0
        ORDER = 2

        def _hyena_filter(L, D, w1, b1, w2, b2, filt_bias, filt_decay):
            t = jnp.linspace(0.0, 1.0, L)[:, None]
            bands = jnp.linspace(0.0, EMB_DIM - 1.0, EMB_DIM)[None, :]
            pe = jnp.sin(t * bands * FREQ)
            h = jnp.sin(FREQ * (pe @ w1.T + b1)) @ w2.T + b2
            h = h.reshape(L, ORDER, D).transpose(1, 2, 0)
            t_window = jnp.linspace(0.0, 1.0, L)[None, None, :]
            decay = jnp.exp(-jnp.exp(filt_decay)[..., None] * t_window)
            h = h * decay + filt_bias[..., None]
            return h * (1.0 / L)

        def _depthwise_conv3(x, w, b):
            xp = jnp.pad(x, ((0, 0), (0, 0), (1, 1)))
            return w[:, 0, None] * xp[:, :, :-2] + w[:, 1, None] * xp[:, :, 1:-1] + w[:, 2, None] * xp[:, :, 2:] + b[:, None]
        key = jax.random.key(seed)
        ks = jax.random.split(key, 8)
        B, L, D = (2, 512, 128)
        OD = (ORDER + 1) * D
        std = 0.02
        return {'u': jax.random.normal(ks[0], (B, L, D), jnp.float32), 'w_in': jax.random.normal(ks[1], (OD, D), jnp.float32) * std, 'b_in': jnp.zeros((OD,), jnp.float32), 'conv_w': jax.random.normal(ks[2], (OD, 3), jnp.float32) * std, 'conv_b': jnp.zeros((OD,), jnp.float32), 'w1': jax.random.normal(ks[3], (64, EMB_DIM), jnp.float32) * std, 'b1': jnp.zeros((64,), jnp.float32), 'w2': jax.random.normal(ks[4], (ORDER * D, 64), jnp.float32) * std, 'b2': jnp.zeros((ORDER * D,), jnp.float32), 'filt_bias': jnp.zeros((ORDER, D), jnp.float32), 'filt_decay': jnp.ones((ORDER, D), jnp.float32) * -3.0, 'w_out': jax.random.normal(ks[5], (D, D), jnp.float32) * std, 'b_out': jnp.zeros((D,), jnp.float32)}
    _L0_attn_in = _L0_attn_setup()

    def _L0_ffn_setup():
        import jax, jax.numpy as jnp
        import numpy as np
        H = 128
        I = 64
        E = 32
        TOP_K = 6
        N_GROUP = 8
        TOPK_GROUP = 4
        SCALE = 2.5
        N_SHARED = 2
        SI = I * N_SHARED
        B, S = (2, 128)
        key = jax.random.key(seed)
        ks = jax.random.split(key, 8)
        x = jax.random.normal(ks[0], (B, S, H), jnp.float32)
        gate_weight = jax.random.normal(ks[1], (E, H), jnp.float32) * 0.02
        e_score_correction_bias = jax.random.normal(ks[2], (E,), jnp.float32) * 0.01
        experts_gate_up = jax.random.normal(ks[3], (E, 2 * I, H), jnp.float32) * 0.02
        experts_down = jax.random.normal(ks[4], (E, H, I), jnp.float32) * 0.02
        shared_gate_w = jax.random.normal(ks[5], (SI, H), jnp.float32) * 0.02
        shared_up_w = jax.random.normal(ks[6], (SI, H), jnp.float32) * 0.02
        shared_down_w = jax.random.normal(ks[7], (H, SI), jnp.float32) * 0.02
        return {'x': x, 'gate_weight': gate_weight, 'e_score_correction_bias': e_score_correction_bias, 'experts_gate_up': experts_gate_up, 'experts_down': experts_down, 'shared_gate_w': shared_gate_w, 'shared_up_w': shared_up_w, 'shared_down_w': shared_down_w}
    _L0_ffn_in = _L0_ffn_setup()
    _L0_c = _w((lambda *s: np.random.randn(*s).astype(np.float32) * 0.05)(4, 128))
    _L0_wmod = _w((lambda *s: np.random.randn(*s).astype(np.float32) * 0.05)(128, 6 * 128) * 128 ** (-0.5))
    _d = {'L0_attn_u': _L0_attn_in['u'], 'L0_attn_w_in': _L0_attn_in['w_in'], 'L0_attn_b_in': _L0_attn_in['b_in'], 'L0_attn_conv_w': _L0_attn_in['conv_w'], 'L0_attn_conv_b': _L0_attn_in['conv_b'], 'L0_attn_w1': _L0_attn_in['w1'], 'L0_attn_b1': _L0_attn_in['b1'], 'L0_attn_w2': _L0_attn_in['w2'], 'L0_attn_b2': _L0_attn_in['b2'], 'L0_attn_filt_bias': _L0_attn_in['filt_bias'], 'L0_attn_filt_decay': _L0_attn_in['filt_decay'], 'L0_attn_w_out': _L0_attn_in['w_out'], 'L0_attn_b_out': _L0_attn_in['b_out'], 'L0_ffn_gate_weight': _L0_ffn_in['gate_weight'], 'L0_ffn_e_score_correction_bias': _L0_ffn_in['e_score_correction_bias'], 'L0_ffn_experts_gate_up': _L0_ffn_in['experts_gate_up'], 'L0_ffn_experts_down': _L0_ffn_in['experts_down'], 'L0_ffn_shared_gate_w': _L0_ffn_in['shared_gate_w'], 'L0_ffn_shared_up_w': _L0_ffn_in['shared_up_w'], 'L0_ffn_shared_down_w': _L0_ffn_in['shared_down_w'], 'L0_c': _L0_c, 'L0_wmod': _L0_wmod}
    _x0 = _d['L0_attn_u']
    _d['L0_attn_u'] = jax.random.normal(jax.random.fold_in(jax.random.key(seed), 1), (4, 512, 128), dtype=_x0.dtype)
    del _x0
    return _d

def reference(L0_attn_u, L0_attn_w_in, L0_attn_b_in, L0_attn_conv_w, L0_attn_conv_b, L0_attn_w1, L0_attn_b1, L0_attn_w2, L0_attn_b2, L0_attn_filt_bias, L0_attn_filt_decay, L0_attn_w_out, L0_attn_b_out, L0_ffn_gate_weight, L0_ffn_e_score_correction_bias, L0_ffn_experts_gate_up, L0_ffn_experts_down, L0_ffn_shared_gate_w, L0_ffn_shared_up_w, L0_ffn_shared_down_w, L0_c, L0_wmod):

    def _L0_attn_ref(u, w_in, b_in, conv_w, conv_b, w1, b1, w2, b2, filt_bias, filt_decay, w_out, b_out):
        import jax, jax.numpy as jnp
        import numpy as np
        EMB_DIM = 33
        FREQ = 10.0
        ORDER = 2

        def _hyena_filter(L, D, w1, b1, w2, b2, filt_bias, filt_decay):
            t = jnp.linspace(0.0, 1.0, L)[:, None]
            bands = jnp.linspace(0.0, EMB_DIM - 1.0, EMB_DIM)[None, :]
            pe = jnp.sin(t * bands * FREQ)
            h = jnp.sin(FREQ * (pe @ w1.T + b1)) @ w2.T + b2
            h = h.reshape(L, ORDER, D).transpose(1, 2, 0)
            t_window = jnp.linspace(0.0, 1.0, L)[None, None, :]
            decay = jnp.exp(-jnp.exp(filt_decay)[..., None] * t_window)
            h = h * decay + filt_bias[..., None]
            return h * (1.0 / L)

        def _depthwise_conv3(x, w, b):
            xp = jnp.pad(x, ((0, 0), (0, 0), (1, 1)))
            return w[:, 0, None] * xp[:, :, :-2] + w[:, 1, None] * xp[:, :, 1:-1] + w[:, 2, None] * xp[:, :, 2:] + b[:, None]
        B, L, D = u.shape
        res = u @ w_in.T + b_in
        res = res.transpose(0, 2, 1)
        res = _depthwise_conv3(res, conv_w, conv_b)
        res = res.reshape(B, ORDER + 1, D, L)
        x = res[:, :-1]
        v = res[:, -1]
        h = _hyena_filter(L, D, w1, b1, w2, b2, filt_bias, filt_decay)
        n_fft = 2 * L
        for n in range(ORDER):
            v_fft = jnp.fft.rfft(v, n=n_fft, axis=-1)
            h_fft = jnp.fft.rfft(h[n], n=n_fft, axis=-1)
            y = jnp.fft.irfft(v_fft * h_fft, n=n_fft, axis=-1)[..., :L]
            v = y * x[:, n]
        return v.transpose(0, 2, 1) @ w_out.T + b_out

    def _L0_ffn_ref(x, gate_weight, e_score_correction_bias, experts_gate_up, experts_down, shared_gate_w, shared_up_w, shared_down_w):
        import jax, jax.numpy as jnp
        import numpy as np
        H = 128
        I = 64
        E = 32
        TOP_K = 6
        N_GROUP = 8
        TOPK_GROUP = 4
        SCALE = 2.5
        N_SHARED = 2
        SI = I * N_SHARED
        B, S = (2, 128)
        b, s, h = x.shape
        xf = x.reshape(-1, h)
        T = xf.shape[0]
        logits = xf.astype(jnp.float32) @ gate_weight.astype(jnp.float32).T
        scores = jax.nn.sigmoid(logits)
        sfc = scores + e_score_correction_bias[None, :]
        gs = E // N_GROUP
        group_scores = sfc.reshape(T, N_GROUP, gs).max(axis=-1)
        _, gidx = jax.lax.top_k(group_scores, TOPK_GROUP)
        gmask = jnp.zeros((T, N_GROUP), bool).at[jnp.arange(T)[:, None], gidx].set(True)
        smask = jnp.repeat(gmask, gs, axis=1)
        masked = jnp.where(smask, sfc, 0.0)
        _, topk_idx = jax.lax.top_k(masked, TOP_K)
        tw = jnp.take_along_axis(scores, topk_idx, axis=1)
        tw = tw / (tw.sum(-1, keepdims=True) + 1e-20)
        tw = (tw * SCALE).astype(xf.dtype)
        combine = jnp.zeros((T, E), xf.dtype).at[jnp.arange(T)[:, None], topk_idx].add(tw)

        def expert_step(acc, inp):
            gu, dn, c = inp
            g = xf @ gu[:I].T
            u = xf @ gu[I:].T
            o = jax.nn.silu(g) * u @ dn.T
            return (acc + c[:, None] * o, None)
        routed, _ = jax.lax.scan(expert_step, jnp.zeros_like(xf), (experts_gate_up, experts_down, combine.T))
        sh = jax.nn.silu(xf @ shared_gate_w.T) * (xf @ shared_up_w.T)
        shared_out = sh @ shared_down_w.T
        return (routed + shared_out).reshape(b, s, h)
    x = L0_attn_u
    mod = (_silu(L0_c) @ L0_wmod).reshape(L0_c.shape[0], 6, 1, -1)
    sa, ca, ga, sb, cb, gb = (mod[:, 0], mod[:, 1], mod[:, 2], mod[:, 3], mod[:, 4], mod[:, 5])
    ga = (2 * (ga >= 0) - 1) * jnp.maximum(jnp.abs(ga), 0.25)
    gb = (2 * (gb >= 0) - 1) * jnp.maximum(jnp.abs(gb), 0.25)
    h = _layernorm(x, axis=-1) * (1 + ca) + sa
    x = x + ga * _L0_attn_ref(h, L0_attn_w_in, L0_attn_b_in, L0_attn_conv_w, L0_attn_conv_b, L0_attn_w1, L0_attn_b1, L0_attn_w2, L0_attn_b2, L0_attn_filt_bias, L0_attn_filt_decay, L0_attn_w_out, L0_attn_b_out)
    h = _layernorm(x, axis=-1) * (1 + cb) + sb
    x = x + gb * _L0_ffn_ref(h, L0_ffn_gate_weight, L0_ffn_e_score_correction_bias, L0_ffn_experts_gate_up, L0_ffn_experts_down, L0_ffn_shared_gate_w, L0_ffn_shared_up_w, L0_ffn_shared_down_w)
    return x

_drawn_inputs = setup_inputs


def setup_inputs(seed=0):
    import zlib

    import numpy as np

    out = dict(_drawn_inputs(seed))
    spreads = {'L0_attn_b_in': (0.0, 0.8),
     'L0_attn_conv_b': (0.0, 0.8),
     'L0_attn_b1': (0.0, 0.8),
     'L0_attn_b2': (0.0, 0.8),
     'L0_attn_filt_bias': (0.0, 0.8),
     'L0_attn_filt_decay': (-3.0, 0.6),
     'L0_attn_b_out': (0.0, 0.34)}
    factors = {'L0_attn_w_in': 8.0,
     'L0_attn_conv_w': 8.0,
     'L0_attn_w1': 8.0,
     'L0_attn_w2': 8.0,
     'L0_attn_w_out': 8.0,
     'L0_ffn_gate_weight': 8.0,
     'L0_ffn_e_score_correction_bias': 8.0,
     'L0_ffn_experts_gate_up': 8.0,
     'L0_ffn_experts_down': 8.0,
     'L0_ffn_shared_gate_w': 8.0,
     'L0_ffn_shared_up_w': 8.0,
     'L0_ffn_shared_down_w': 8.0}
    for name, (base, spread) in spreads.items():
        noise = np.random.default_rng([zlib.crc32(name.encode()), seed]).standard_normal(out[name].shape)
        drawn = base * np.exp(spread * noise) if base else spread * noise
        out[name] = jnp.asarray(drawn.astype(out[name].dtype))
    for name, factor in factors.items():
        out[name] = (out[name] * factor).astype(out[name].dtype)
    return out
```

```python
from contextlib import ExitStack

import concourse.bass as bass
import numpy as np
from concourse import mybir

F32 = mybir.dt.float32
F32R = mybir.dt.float32r
U32 = mybir.dt.uint32
ALU = mybir.AluOpType
ACT = mybir.ActivationFunctionType
AX_X = mybir.AxisListType.X

P = 128
B, L, D = 4, 512, 128
NJ = L // P
NT = B * NJ
ORDER = 2
GROUPS = ORDER + 1
EMB, HID = 33, 64
E, TOP_K, N_GROUP, TOPK_GROUP = 32, 6, 8, 4
GS = E // N_GROUP
ROUTED_SCALE = 2.5
INTER = 64
PAIRS = E // 2
NU = PAIRS + 1
EPS = 1e-5
MAX8 = 8
BIG = 3.0e38
FREQ = 10.0
ROUND = 1.5 * 2.0 ** 23
TWO_PI = (6.28125, 1.9340515136718750e-03, 1.2556659146298881e-06)
PI = 3.1415925
READY = 1
CHUNK = 2


def build(nc, io, out):
    ctx = ExitStack()
    with ctx:
        def sem(name):
            return ctx.enter_context(nc.semaphore(name))

        def sb(name, shape, dt=F32):
            return ctx.enter_context(nc.sbuf_tensor(name, shape, dt))

        def overlay(region, *groups):
            got, most = {}, 0
            for group in groups:
                with ExitStack() as inner:
                    words = 0
                    for name, shape, dt in group:
                        got[name] = inner.enter_context(nc.sbuf_tensor(name, shape, dt))
                        words += int(np.prod(shape[1:]))
                    most = max(most, words)
            sb(region, [P, most + 16])
            return got

        bank = [ctx.enter_context(nc.psum_tensor(f"bank{i}", [P, 512], F32)) for i in range(8)]

        x = sb("x", [P, B, NJ, D])
        dft_hi = sb("dft_hi", [P, 2, NJ, L], F32R)
        dft_lo = sb("dft_lo", [P, 2, NJ, L], F32R)
        w_hi = sb("w_hi", [P, NU, 3, D], F32R)
        w_lo = sb("w_lo", [P, NU, 3, D], F32R)
        v = sb("v", [P, B, L])
        tok_hi = sb("tok_hi", [P, NJ, B, D], F32R)
        tok_lo = sb("tok_lo", [P, NJ, B, D], F32R)
        w_stage = sb("w_stage", [P, 2, CHUNK, 3, D])
        ident = sb("ident", [P, P])
        w_out_t = sb("w_out_t", [P, D])
        w_out_g = sb("w_out_g", [P, B, D])
        gate_w_t = sb("gate_w_t", [P, E])
        cols = sb("cols", [P, 15])
        conv_bias = sb("conv_bias", [P, GROUPS])
        consts = sb("consts", [P, 16])
        rows = sb("rows", [P, 672])
        modT = sb("modT", [P, 6, B])
        stats = sb("stats", [P, NT, 6])
        mv = sb("mv", [P, NT, 2])
        var_eps = sb("var_eps", [P, NT])
        sd = sb("sd", [P, NT])
        rstd = sb("rstd", [P, NT])
        newton = sb("newton", [P, NT])
        c_t = sb("c_t", [P, B])
        silu_c = sb("silu_c", [P, B])
        sign = sb("sign", [P, B])

        big = overlay(
            "region_spectra",
            [("dft_raw", [P, 2, NJ, L], F32), ("h_t", [P, B, L], F32), ("decay", [P, NJ, ORDER * D], F32),
             ("wmod", [P, 6 * D], F32)],
            [("y_hi", [P, 2, NJ, B * D], F32R), ("y_lo", [P, 2, NJ, B * D], F32R)],
            [("silu_g", [P, 2, L], F32), ("gated", [P, 2, L], F32), ("act", [P, 2, L], F32),
             ("act_hi", [P, 3, L], F32R), ("act_lo", [P, 3, L], F32R), ("moe_t", [P, L], F32),
             ("out_tok", [P, NJ, D], F32)],
            [("pick_raw", [2 * E, PAIRS, P], F32)],
        )
        mid = overlay(
            "region_gates",
            [("gates", [P, ORDER, B, L], F32)],
            [("xhat", [P, NT, D], F32), ("comb_t", [2 * E, NT * P], F32R)],
        )
        gates, xhat, comb_t = (mid[k] for k in ("gates", "xhat", "comb_t"))
        small = overlay(
            "region_products",
            [("padded", [P, 2, L + 2], F32), ("silu_rep", [P, B, P], F32), ("ga", [P, B, D], F32),
             ("ga_sign", [P, B, D], F32), ("turns", [HID, L], F32), ("angle", [HID, L], F32)],
            [("prod", [P, 4, B * D], F32), ("y", [P, 2, 2, B * D], F32)],
            [("scores", [P, NT, E], F32), ("biased", [P, NT, E], F32), ("group_max", [P, NT, N_GROUP + TOPK_GROUP], F32),
             ("group_left", [P, NT, N_GROUP + TOPK_GROUP], F32), ("group_in", [P, NT, N_GROUP], F32),
             ("masked", [P, NT, E + 2], F32), ("left", [P, NT, E + 2], F32), ("top8", [P, NT, MAX8], F32),
             ("weight_sum", [P, NT], F32), ("comb", [P, NT, 2, E], F32R)],
        )
        filt = overlay(
            "region_filter",
            [("pos_t", [EMB + 1, L], F32), ("w1a", [EMB + 1, HID], F32), ("w2a", [HID + 1, ORDER * D], F32),
             ("w_in_t", [P, GROUPS * D], F32), ("wave", [HID + 1, L], F32)],
            [("filt_c", [P, ORDER, NJ, D], F32), ("filt_s", [P, ORDER, NJ, D], F32)],
            [("pick", [2 * E, PAIRS, P], F32R)],
        )
        filt_c, filt_s, pick = filt["filt_c"], filt["filt_s"], filt["pick"]
        dft_raw, h_t, decay, wmod, y_hi, y_lo = (big[k] for k in ("dft_raw", "h_t", "decay", "wmod", "y_hi", "y_lo"))
        silu_g, gated, act, act_hi, act_lo = (big[k] for k in ("silu_g", "gated", "act", "act_hi", "act_lo"))
        moe_t, out_tok, pick_raw = (big[k] for k in ("moe_t", "out_tok", "pick_raw"))
        padded, silu_rep, ga, ga_sign, turns, angle = (
            small[k] for k in ("padded", "silu_rep", "ga", "ga_sign", "turns", "angle"))
        prod, y = small["prod"], small["y"]
        scores, biased, group_max, group_left, group_in = (
            small[k] for k in ("scores", "biased", "group_max", "group_left", "group_in"))
        masked, left, top8, weight_sum, comb = (small[k] for k in ("masked", "left", "top8", "weight_sum", "comb"))
        pos_t, w1a, w2a, w_in_t, wave = (filt[k] for k in ("pos_t", "w1a", "w2a", "w_in_t", "wave"))

        h_hi = tok_hi[:].rearrange("p j b d -> p (j b d)")[:, 0:NJ * ORDER * D].rearrange("p (j c) -> p j c", j=NJ)
        h_lo = tok_lo[:].rearrange("p j b d -> p (j b d)")[:, 0:NJ * ORDER * D].rearrange("p (j c) -> p j c", j=NJ)
        h_time = decay
        x_tiles = x[:].rearrange("p b j d -> p (b j) d")
        h2 = v
        h2_hi = tok_hi[:].rearrange("p j b d -> p (j b d)").rearrange("p (b l) -> p b l", b=B)
        h2_lo = tok_lo[:].rearrange("p j b d -> p (j b d)").rearrange("p (b l) -> p b l", b=B)
        SA, CA, GA, SB, CB, GB = range(6)
        DECAY, FBIAS, BOUT, CORR = slice(0, 256), slice(256, 512), slice(512, 640), slice(640, 672)

        mod_in, filt_in, const_in, proj_in, late_in, pick_in = (
            sem(n) for n in ("mod_in", "filt_in", "const_in", "proj_in", "late_in", "pick_in"))
        x_in = [sem(f"x_in{b}") for b in range(B)]
        dft_in = [sem(f"dft_in{i}") for i in range(2)]
        n_chunks = -(-NU // CHUNK)
        w_in_sem = [sem(f"w_in{i}") for i in range(2)]
        silu_c_done, rep_done, mod_mm, ga_mm, mod_done, ga_done, zero_done = (
            sem(n) for n in ("silu_c_done", "rep_done", "mod_mm", "ga_mm", "mod_done", "ga_done", "zero_done"))
        var_done, sd_done, xhat_done, xhat_t, h_t_done = (
            sem(n) for n in ("var_done", "sd_done", "xhat_done", "xhat_t", "h_t_done"))
        proj_mm, padded_done, mid_done, gates_done, v_done = (
            sem(n) for n in ("proj_mm", "padded_done", "mid_done", "gates_done", "v_done"))
        z_mm, angle_in, angle_done, wave_done, decay_done, h_mm, h_done, h_hi_done, h_lo_done, hs_mm, hs_used = (
            sem(n) for n in ("z_mm", "angle_in", "angle_done", "wave_done", "decay_done", "h_mm", "h_done",
                             "h_hi_done", "h_lo_done", "hs_mm", "hs_used"))
        dft_hi_done, dft_lo_done, w_hi_done, w_lo_done, pick_done = (
            sem(n) for n in ("dft_hi_done", "dft_lo_done", "w_hi_done", "w_lo_done", "pick_done"))
        v_t, tok_hi_done, tok_lo_done, spec_mm, prod_done, y_done, y_hi_done, y_lo_done, inv_mm = (
            sem(n) for n in ("v_t", "tok_hi_done", "tok_lo_done", "spec_mm", "prod_done", "y_done", "y_hi_done",
                             "y_lo_done", "inv_mm"))
        attn_mm, x1_done, h2_done, h2_hi_done, h2_lo_done, logits_mm, scores_done, comb_done, comb_tr, comb_t_done = (
            sem(n) for n in ("attn_mm", "x1_done", "h2_done", "h2_hi_done", "h2_lo_done", "logits_mm", "scores_done",
                             "comb_done", "comb_tr", "comb_t_done"))
        gate_mm, up_mm, weight_mm, down_mm, silu_done, gated_done, act_done, act_hi_done, act_lo_done = (
            sem(n) for n in ("gate_mm", "up_mm", "weight_mm", "down_mm", "silu_done", "gated_done", "act_done",
                             "act_hi_done", "act_lo_done"))
        moe_done, moe_tr, out_done, stored = (sem(n) for n in ("moe_done", "moe_tr", "out_done", "stored"))
        dve_chain, act_chain = sem("dve_chain"), sem("act_chain")

        block = ctx.enter_context(nc.Block())

        def chunk_units(q):
            return q * CHUNK, min(NU, (q + 1) * CHUNK)

        @block.sync
        def _(sp):
            sp.dma_start(c_t[:], io["c_t"]).then_inc(mod_in, 16)
            sp.dma_start(wmod[:], io["wmod"]).then_inc(mod_in, 16)
            sp.dma_start(w1a[:], io["w1a"]).then_inc(filt_in, 16)
            sp.dma_start(pos_t[:], io["pos_t"]).then_inc(filt_in, 16)
            sp.dma_start(w2a[:], io["w2a"]).then_inc(filt_in, 16)
            sp.dma_start(ident[:], io["ident"]).then_inc(proj_in, 16)
            sp.dma_start(w_in_t[:], io["w_in_t"]).then_inc(proj_in, 16)
            sp.dma_start(cols[:], io["cols"]).then_inc(proj_in, 16)
            sp.dma_start(w_out_t[:], io["w_out_t"]).then_inc(proj_in, 16)
            for b in range(B):
                sp.dma_start(x[:, b], io["x"][b].rearrange("(j p) d -> p j d", p=P)).then_inc(x_in[b], 16)
            sp.dma_start(rows[:], io["rows"].rearrange("(a n) -> a n", a=1).to_broadcast([P, 672])).then_inc(const_in, 16)
            sp.dma_start(consts[:], io["consts"]).then_inc(const_in, 16)
            for i in range(2):
                sp.dma_start(dft_raw[:, i], io["dft"][:, i]).then_inc(dft_in[i], 16)
            sp.dma_start(gate_w_t[:], io["gate_w_t"]).then_inc(late_in, 16)
            for q in range(n_chunks):
                a, z = chunk_units(q)
                if q >= 2:
                    sp.wait_ge(w_lo_done, q - 1)
                sp.dma_start(w_stage[:, q % 2, 0:z - a], io["w_experts"][:, a:z]).then_inc(w_in_sem[q % 2], 16)
            sp.wait_ge(inv_mm, ORDER * B)
            sp.dma_start(pick_raw[:], io["pick"]).then_inc(pick_in, 16)
            nc.sync.sem_inc(stored, READY)
            with sp.Fori(0, B) as b:
                sp.wait_ge(out_done, READY + b + 1)
                sp.dma_start(out[bass.ds(b, 1)].rearrange("o (j p) d -> p (o j) d", p=P), out_tok[:]).then_inc(stored, 16)
            sp.wait_ge(stored, READY + 16 * B)

        @block.gpsimd
        def _(pool):
            for i in range(2):
                pool.wait_ge(dft_hi_done, i + 1)
                nc.gpsimd.tensor_tensor(dft_lo[:, i], dft_raw[:, i], dft_hi[:, i].bitcast(F32),
                                        ALU.subtract).then_inc(dft_lo_done, 1)
            for q in range(n_chunks):
                a, z = chunk_units(q)
                pool.wait_ge(w_hi_done, q + 1)
                nc.gpsimd.tensor_tensor(w_lo[:, a:z], w_stage[:, q % 2, 0:z - a], w_hi[:, a:z].bitcast(F32),
                                        ALU.subtract).then_inc(w_lo_done, 1)
            with pool.Fori(0, ORDER) as n:
                for kt in range(NJ):
                    for part in range(2):
                        pool.wait_ge(y_hi_done, 8 * n + 2 * kt + part + 1)
                        nc.gpsimd.tensor_tensor(y_lo[:, part, kt], y[:, kt % 2, part],
                                                y_hi[:, part, kt].bitcast(F32), ALU.subtract).then_inc(y_lo_done, 1)
            for b in range(B):
                pool.wait_ge(h2_hi_done, b + 1)
                nc.gpsimd.tensor_tensor(h2_lo[:, b], h2[:, b], h2_hi[:, b].bitcast(F32),
                                        ALU.subtract).then_inc(h2_lo_done, 1)
            nc.gpsimd.sem_inc(act_lo_done, READY)
            with pool.Fori(0, B) as b:
                for u in range(NU):
                    pool.wait_ge(act_hi_done, NU * b + u + 1)
                    nc.gpsimd.tensor_tensor(act_lo[:, u % 3], act[:, u % 2], act_hi[:, u % 3].bitcast(F32),
                                            ALU.subtract).then_inc(act_lo_done, 1)

        @block.scalar
        def _(act_e):
            sc = nc.scalar
            act_e.wait_ge(mod_in, 32)
            sc.activation(silu_c[:], c_t[:], ACT.Silu).then_inc(silu_c_done, 1)
            act_e.wait_ge(z_mm, 1)
            sc.activation(angle[:], bank[6][0:HID, :], ACT.Copy, scale=FREQ).then_inc(angle_in, 1)
            act_e.wait_ge(angle_done, 1)
            sc.activation(wave[0:HID], angle[:], ACT.Sin).then_inc(wave_done, 1)
            act_e.wait_ge(const_in, 32)
            sc.activation(rows[:, DECAY], rows[:, DECAY], ACT.Exp).then_inc(act_chain, 1)
            act_e.wait_ge(act_chain, 1)
            for j in range(NJ):
                sc.activation(decay[:, j], rows[:, DECAY], ACT.Exp, scale=consts[:, j:j + 1]).then_inc(decay_done, 1)
            act_e.wait_ge(var_done, 1)
            sc.activation(sd[:], var_eps[:], ACT.Sqrt).then_inc(sd_done, 1)
            for i in range(2):
                act_e.wait_ge(dft_in[i], 16)
                sc.activation(dft_hi[:, i], dft_raw[:, i], ACT.Copy).then_inc(dft_hi_done, 1)
            act_e.wait_ge(mod_done, 1)
            for b in range(B):
                act_e.wait_ge(xhat_t, b + 1)
                sc.activation(h_t[:, b], bank[b % 2][:], ACT.Identity, bias=modT[:, SA, b:b + 1],
                              scale=modT[:, CA, b:b + 1]).then_inc(h_t_done, 1)
            act_e.wait_ge(zero_done, 1)
            for m in range(GROUPS * B):
                g, b = (GROUPS - 1, m) if m < B else ((m - B) // B, m % B)
                dst = v[:, b] if g == GROUPS - 1 else gates[:, g, b]
                act_e.wait_ge(proj_mm, m + 1)
                if m >= 2:
                    act_e.wait_ge(*((v_done, m - 1) if m - 2 < B else (gates_done, m - 1 - B)))
                sc.activation(padded[:, m % 2, 1:L + 1], bank[2 + m % 4][:], ACT.Identity,
                              bias=cols[:, g:g + 1]).then_inc(padded_done, 1)
                sc.activation(dst, bank[2 + m % 4][:], ACT.Identity, bias=conv_bias[:, g:g + 1],
                              scale=cols[:, 6 + g:7 + g]).then_inc(mid_done, 1)
            act_e.wait_ge(h_done, 1)
            sc.activation(h_hi, h_time[:], ACT.Copy).then_inc(h_hi_done, 1)
            for q in range(n_chunks):
                a, z = chunk_units(q)
                act_e.wait_ge(w_in_sem[q % 2], 16 * (q // 2 + 1))
                sc.activation(w_hi[:, a:z], w_stage[:, q % 2, 0:z - a], ACT.Copy).then_inc(w_hi_done, 1)
            with act_e.Fori(0, ORDER) as n:
                for b in range(B):
                    act_e.wait_ge(v_t, 4 * n + b + 1)
                    sc.activation(tok_hi[:, :, b], bank[b % 2][:].rearrange("p (j d) -> p j d", j=NJ),
                                  ACT.Copy).then_inc(tok_hi_done, 1)
                for kt in range(NJ):
                    for part in range(2):
                        act_e.wait_ge(y_done, 8 * n + 2 * kt + part + 1)
                        sc.activation(y_hi[:, part, kt], y[:, kt % 2, part], ACT.Copy).then_inc(y_hi_done, 1)
            act_e.wait_ge(pick_in, 16)
            sc.activation(pick[:], pick_raw[:], ACT.Copy).then_inc(pick_done, 1)
            act_e.wait_ge(var_done, 2)
            sc.activation(sd[:], var_eps[:], ACT.Sqrt).then_inc(sd_done, 1)
            for b in range(B):
                act_e.wait_ge(xhat_t, B + b + 1)
                sc.activation(h2[:, b], bank[b % 2][:], ACT.Identity, bias=modT[:, SB, b:b + 1],
                              scale=modT[:, CB, b:b + 1]).then_inc(h2_done, 1)
                act_e.wait_ge(h2_done, b + 1)
                sc.activation(h2_hi[:, b], h2[:, b], ACT.Copy).then_inc(h2_hi_done, 1)
            act_e.wait_ge(logits_mm, 1)
            sc.activation(scores[:].rearrange("p t e -> p (t e)"), bank[2][:], ACT.Sigmoid).then_inc(scores_done, 1)
            for b in range(B):
                act_e.wait_ge(comb_tr, b + 1)
                sc.activation(comb_t[:, b * L:(b + 1) * L], bank[4 + b % 2][0:2 * E, :], ACT.Copy).then_inc(comb_t_done, 1)
            sc.sem_inc(moe_done, READY)
            with act_e.Fori(0, B) as b:
                for u in range(NU + 1):
                    if u < NU:
                        act_e.wait_ge(gate_mm, NU * b + u + 1)
                        if u == 0:
                            act_e.wait_ge(act_done, READY + NU * b)
                        if u >= 2:
                            act_e.wait_ge(gated_done, PAIRS * b + u - 1)
                        sc.activation(silu_g[:, u % 2], bank[u % 2][:], ACT.Silu).then_inc(silu_done, 1)
                    if u >= 1:
                        d = u - 1
                        act_e.wait_ge(act_done, READY + NU * b + d + 1)
                        if d == 0:
                            act_e.wait_ge(down_mm, READY + NU * b)
                        if d >= 3:
                            act_e.wait_ge(down_mm, READY + NU * b + d - 2)
                        sc.activation(act_hi[:, d % 3], act[:, d % 2], ACT.Copy).then_inc(act_hi_done, 1)
                act_e.wait_ge(down_mm, READY + NU * b + NU)
                act_e.wait_ge(moe_tr, READY + b)
                sc.activation(moe_t[:], bank[6][:], ACT.Copy, scale=modT[:, GB, bass.ds(b, 1)]).then_inc(moe_done, 1)

        @block.vector
        def _(dve):
            ve = nc.vector
            chain = [0]

            def link(ins):
                chain[0] += 1
                ins.then_inc(dve_chain, 1)
                dve.wait_ge(dve_chain, chain[0])

            def norm_stats(done):
                link(ve.tensor_scalar(var_eps[:], mv[:, :, 1], EPS, None, ALU.add))
                ve.tensor_copy(newton[:], var_eps[:]).then_inc(var_done, 1)
                dve.wait_ge(sd_done, done)
                link(ve.reciprocal(rstd[:], sd[:]))
                link(ve.tensor_tensor(newton[:], rstd[:], rstd[:], ALU.mult))
                link(ve.tensor_tensor(newton[:], newton[:], var_eps[:], ALU.mult))
                link(ve.tensor_scalar(newton[:], newton[:], -0.5, 1.5, ALU.mult, ALU.add))
                link(ve.tensor_tensor(rstd[:], rstd[:], newton[:], ALU.mult))

            def normalise():
                for b in range(B):
                    for t in range(b * NJ, (b + 1) * NJ):
                        last = ve.tensor_scalar(xhat[:, t], x_tiles[:, t], mv[:, t, 0:1], rstd[:, t:t + 1],
                                                ALU.subtract, ALU.mult)
                    last.then_inc(xhat_done, 1)

            ve.memset(padded[:], 0.0).then_inc(zero_done, 1)
            ve.memset(wave[HID:HID + 1], 1.0)
            dve.wait_ge(silu_c_done, 1)
            ve.tensor_copy(silu_rep[:], silu_c[:].unsqueeze(2).to_broadcast([P, B, P])).then_inc(rep_done, 1)
            dve.wait_ge(mod_mm, 1)
            link(ve.tensor_copy(modT[:].rearrange("p m b -> p (m b)"), bank[6][:, 0:6 * B]))
            ve.tensor_scalar(modT[:, CA], modT[:, CA], 1.0, None, ALU.add)
            ve.tensor_scalar(modT[:, CB], modT[:, CB], 1.0, None, ALU.add)
            dve.wait_ge(proj_in, 64)
            ve.tensor_tensor(conv_bias[:], cols[:, 0:3], cols[:, 6:9], ALU.mult)
            link(ve.tensor_scalar(sign[:], modT[:, GB], 0.0, 2.0, ALU.is_ge, ALU.mult))
            ve.tensor_tensor(conv_bias[:], conv_bias[:], cols[:, 12:15], ALU.add)
            link(ve.tensor_scalar(sign[:], sign[:], -1.0, None, ALU.add))
            link(ve.tensor_tensor(modT[:, GB], modT[:, GB], sign[:], ALU.mult))
            ve.scalar_tensor_tensor(modT[:, GB], modT[:, GB], 0.25, sign[:], ALU.max, ALU.mult).then_inc(mod_done, 1)
            dve.wait_ge(angle_in, 1)
            link(ve.tensor_scalar(turns[:], angle[:], float(1 / (2 * np.pi)), ROUND, ALU.mult, ALU.add))
            link(ve.tensor_scalar(turns[:], turns[:], -ROUND, None, ALU.add))
            for part in TWO_PI:
                link(ve.scalar_tensor_tensor(angle[:], turns[:], -part, angle[:], ALU.mult, ALU.add))
            ve.tensor_scalar(angle[:], angle[:], PI, -PI, ALU.min, ALU.max).then_inc(angle_done, 1)
            for b in range(B):
                dve.wait_ge(x_in[b], 16)
                for t in range(b * NJ, (b + 1) * NJ):
                    last = ve.bn_stats(stats[:, t], x_tiles[:, t])
            link(last)
            for t in range(NT):
                last = ve.bn_aggr(mv[:, t], stats[:, t])
            link(last)
            norm_stats(1)
            normalise()
            dve.wait_ge(ga_mm, 1)
            ga_flat = ga[:].rearrange("p b d -> p (b d)")
            sign_flat = ga_sign[:].rearrange("p b d -> p (b d)")
            link(ve.tensor_scalar(sign_flat, bank[7][:], 0.0, 2.0, ALU.is_ge, ALU.mult))
            link(ve.tensor_scalar(sign_flat, sign_flat, -1.0, None, ALU.add))
            link(ve.tensor_tensor(ga_flat, bank[7][:], sign_flat, ALU.mult))
            link(ve.scalar_tensor_tensor(ga_flat, ga_flat, 0.25, sign_flat, ALU.max, ALU.mult))
            dve.wait_ge(const_in, 32)
            ve.tensor_tensor(w_out_g[:], ga[:], w_out_t[:].unsqueeze(1).to_broadcast([P, B, D]), ALU.mult)
            link(ve.tensor_tensor(ga[:], ga[:], rows[:, BOUT].unsqueeze(1).to_broadcast([P, B, D]), ALU.mult))
            for b in range(B):
                last = ve.tensor_tensor(x[:, b], x[:, b], ga[:, b].unsqueeze(1).to_broadcast([P, NJ, D]), ALU.add)
            last.then_inc(ga_done, 1)
            for m in range(GROUPS * B):
                g, b = (GROUPS - 1, m) if m < B else ((m - B) // B, m % B)
                dst = v[:, b] if g == GROUPS - 1 else gates[:, g, b]
                dve.wait_ge(mid_done, m + 1)
                link(ve.scalar_tensor_tensor(dst, padded[:, m % 2, 0:L], cols[:, 3 + g:4 + g], dst, ALU.mult, ALU.add))
                last = ve.scalar_tensor_tensor(dst, padded[:, m % 2, 2:L + 2], cols[:, 9 + g:10 + g], dst,
                                               ALU.mult, ALU.add)
                last.then_inc(v_done if m < B else gates_done, 1)
            for j in range(NJ):
                dve.wait_ge(h_mm, j // 2 + 1)
                dve.wait_ge(decay_done, j + 1)
                link(ve.tensor_tensor(h_time[:, j], bank[6 + j // 2][:, (j % 2) * 256:(j % 2 + 1) * 256], decay[:, j],
                                      ALU.mult))
                last = ve.tensor_tensor(h_time[:, j], h_time[:, j], rows[:, FBIAS], ALU.add)
            last.then_inc(h_done, 1)
            dve.wait_ge(h_hi_done, 1)
            ve.tensor_tensor(h_lo, h_time[:], h_hi.bitcast(F32), ALU.subtract).then_inc(h_lo_done, 1)
            for kt in range(NJ):
                dve.wait_ge(hs_mm, kt + 1)
                hc, hs = bank[6 + kt % 2][:, 0:256], bank[6 + kt % 2][:, 256:512]
                cos, sin, neg = (consts[:, 4 * i + kt:4 * i + kt + 1] for i in (1, 2, 3))
                dst_c = filt_c[:, :, kt]
                dst_s = filt_s[:, :, kt]
                two = lambda a: a.rearrange("p (n d) -> p n d", n=ORDER)
                ve.tensor_scalar(dst_c, two(hc), cos, None, ALU.mult)
                link(ve.tensor_scalar(dst_s, two(hs), cos, None, ALU.mult))
                ve.scalar_tensor_tensor(dst_c, two(hs), sin, dst_c, ALU.mult, ALU.add)
                ve.scalar_tensor_tensor(dst_s, two(hc), neg, dst_s, ALU.mult, ALU.add).then_inc(hs_used, 1)
            dve.wait_ge(hs_used, NJ)
            with dve.Fori(0, ORDER) as n:
                for b in range(B):
                    dve.wait_ge(tok_hi_done, 4 * n + b + 1)
                    ve.tensor_tensor(tok_lo[:, :, b], bank[b % 2][:].rearrange("p (j d) -> p j d", j=NJ),
                                     tok_hi[:, :, b].bitcast(F32), ALU.subtract).then_inc(tok_lo_done, 1)
                for kt in range(NJ):
                    vc = bank[2 + 2 * (kt % 2)][:].rearrange("p (b d) -> p b d", b=B)
                    vs = bank[3 + 2 * (kt % 2)][:].rearrange("p (b d) -> p b d", b=B)
                    fc = filt_c[:, bass.ds(n, 1), kt].to_broadcast([P, B, D])
                    fs = filt_s[:, bass.ds(n, 1), kt].to_broadcast([P, B, D])
                    pr = lambda i: prod[:, i].rearrange("p (b d) -> p b d", b=B)
                    dve.wait_ge(spec_mm, 8 * n + 2 * kt + 2)
                    if kt >= 1:
                        dve.wait_ge(y_done, 8 * n + 2 * kt)
                    ve.tensor_tensor(pr(0), vc, fc, ALU.mult)
                    ve.tensor_tensor(pr(1), vs, fs, ALU.mult).then_inc(prod_done, 1)
                    ve.tensor_tensor(pr(2), vs, fc, ALU.mult)
                    ve.tensor_tensor(pr(3), vc, fs, ALU.mult).then_inc(prod_done, 1)
                    if kt >= 2:
                        dve.wait_ge(y_lo_done, 8 * n + 2 * kt - 2)
                    dve.wait_ge(prod_done, 8 * n + 2 * kt + 1)
                    ve.tensor_tensor(y[:, kt % 2, 0], prod[:, 0], prod[:, 1], ALU.subtract).then_inc(y_done, 1)
                    dve.wait_ge(prod_done, 8 * n + 2 * kt + 2)
                    ve.tensor_tensor(y[:, kt % 2, 1], prod[:, 2], prod[:, 3], ALU.add).then_inc(y_done, 1)
                for b in range(B):
                    dve.wait_ge(inv_mm, 4 * n + b + 1)
                    ve.tensor_tensor(v[:, b], bank[6 + b % 2][:], gates[:, bass.ds(n, 1), b].rearrange("p o l -> p (o l)"),
                                     ALU.mult).then_inc(v_done, 1)
            for b in range(B):
                dve.wait_ge(attn_mm, b + 1)
                ve.tensor_tensor(x[:, b].rearrange("p j d -> p (j d)"), bank[2 + b][:],
                                 x[:, b].rearrange("p j d -> p (j d)"), ALU.add).then_inc(x1_done, 1)
            for b in range(B):
                dve.wait_ge(x1_done, b + 1)
                for t in range(b * NJ, (b + 1) * NJ):
                    last = ve.bn_stats(stats[:, t], x_tiles[:, t])
            link(last)
            for t in range(NT):
                last = ve.bn_aggr(mv[:, t], stats[:, t])
            link(last)
            norm_stats(2)
            normalise()
            ve.memset(group_max[:], BIG)
            ve.memset(masked[:, :, 0:E], 0.0)
            link(ve.memset(masked[:, :, E:E + 2], BIG))
            dve.wait_ge(scores_done, 1)
            link(ve.tensor_tensor(biased[:], scores[:], rows[:, CORR].unsqueeze(1).to_broadcast([P, NT, E]), ALU.add))
            link(ve.tensor_reduce(group_max[:, :, 0:N_GROUP], biased[:].rearrange("p t (g s) -> p t g s", g=N_GROUP),
                                  AX_X, ALU.max))
            for t in range(NT):
                last = ve.max(top8[:, t], group_max[:, t])
            link(last)
            for t in range(NT):
                last = ve.match_replace(group_left[:, t], top8[:, t], group_max[:, t], -BIG)
            link(last)
            link(ve.tensor_scalar(group_in[:], group_left[:, :, 0:N_GROUP], -BIG, None, ALU.is_equal))
            for s in range(GS):
                last = ve.copy_predicated(masked[:, :, s:E:GS], group_in[:].bitcast(U32), biased[:, :, s:E:GS])
            link(last)
            for t in range(NT):
                last = ve.max(top8[:, t], masked[:, t])
            link(last)
            for t in range(NT):
                last = ve.match_replace(left[:, t], top8[:, t], masked[:, t], -BIG)
            link(last)
            link(ve.tensor_scalar(left[:, :, 0:E], left[:, :, 0:E], -BIG, None, ALU.is_equal))
            link(ve.tensor_tensor(scores[:], scores[:], left[:, :, 0:E], ALU.mult))
            link(ve.tensor_reduce(weight_sum[:], scores[:], AX_X, ALU.add))
            link(ve.tensor_scalar(weight_sum[:], weight_sum[:], 1e-20, None, ALU.add))
            link(ve.reciprocal(weight_sum[:], weight_sum[:]))
            link(ve.tensor_tensor(scores[:], scores[:], weight_sum[:].unsqueeze(2).to_broadcast([P, NT, E]), ALU.mult))
            link(ve.tensor_scalar(scores[:], scores[:], ROUTED_SCALE, None, ALU.mult))
            link(ve.tensor_copy(comb[:, :, 0], scores[:]))
            ve.tensor_tensor(comb[:, :, 1], scores[:], comb[:, :, 0].bitcast(F32), ALU.subtract).then_inc(comb_done, 1)
            ve.sem_inc(act_done, READY)
            ve.sem_inc(out_done, READY)
            with dve.Fori(0, B) as b:
                for u in range(NU + 1):
                    if u < NU:
                        dve.wait_ge(silu_done, NU * b + u + 1)
                        dve.wait_ge(up_mm, NU * b + u + 1)
                    if u < PAIRS:
                        if u == 0:
                            dve.wait_ge(act_done, READY + NU * b)
                        if u >= 2:
                            dve.wait_ge(act_done, READY + NU * b + u - 1)
                        ve.tensor_tensor(gated[:, u % 2], bank[2 + u % 2][:], silu_g[:, u % 2],
                                         ALU.mult).then_inc(gated_done, 1)
                    if 1 <= u <= PAIRS:
                        d = u - 1
                        dve.wait_ge(gated_done, PAIRS * b + d + 1)
                        dve.wait_ge(weight_mm, PAIRS * b + d + 1)
                        if d == 0:
                            dve.wait_ge(act_lo_done, READY + NU * b)
                        if d >= 2:
                            dve.wait_ge(act_lo_done, READY + NU * b + d - 1)
                        ve.tensor_tensor(act[:, d % 2], bank[4 + d % 2][:], gated[:, d % 2],
                                         ALU.mult).then_inc(act_done, 1)
                    if u == PAIRS:
                        dve.wait_ge(act_lo_done, READY + NU * b + u - 1)
                        ve.tensor_tensor(act[:, u % 2], bank[2 + u % 2][:], silu_g[:, u % 2],
                                         ALU.mult).then_inc(act_done, 1)
                dve.wait_ge(moe_tr, READY + b + 1)
                dve.wait_ge(stored, READY + 16 * b)
                ve.tensor_tensor(out_tok[:].rearrange("p j d -> p (j d)"), bank[7][:],
                                 x[:, bass.ds(b, 1)].rearrange("p o j d -> p (o j d)"), ALU.add).then_inc(out_done, 1)

        @block.tensor
        def _(pe):
            te = nc.tensor

            def three(dst, stat, mov, start, stop):
                (sh, sl), (mh, ml) = stat, mov
                te.matmul(dst, sl, mh, start=start, stop=False)
                te.matmul(dst, sh, ml, start=False, stop=False)
                return te.matmul(dst, sh, mh, start=False, stop=stop)

            def halves(hi, lo, *at):
                return hi[at], lo[at]

            pe.wait_ge(mod_in, 32)
            pe.wait_ge(silu_c_done, 1)
            for m in range(6):
                last = te.matmul(bank[6][:, m * B:(m + 1) * B], wmod[:, m * D:(m + 1) * D], silu_c[:], start=True, stop=True)
            last.then_inc(mod_mm, 1)
            pe.wait_ge(rep_done, 1)
            for b in range(B):
                last = te.matmul(bank[7][:, b * D:(b + 1) * D], silu_rep[:, b], wmod[:, GA * D:(GA + 1) * D],
                                 start=True, stop=True)
            last.then_inc(ga_mm, 1)
            pe.wait_ge(filt_in, 48)
            pe.wait_ge(mod_done, 1)
            te.matmul(bank[6][0:HID, :], w1a[:], pos_t[:], start=True, stop=True).then_inc(z_mm, 1)
            pe.wait_ge(proj_in, 64)

            def turn_norm(first):
                for b in range(B):
                    pe.wait_ge(xhat_done, first * B + b + 1)
                    if b >= 2:
                        pe.wait_ge(h2_done if first else h_t_done, b - 1)
                    for j in range(NJ):
                        last = te.transpose(bank[b % 2][:, j * P:(j + 1) * P], xhat[:, b * NJ + j], ident[:])
                    last.then_inc(xhat_t, 1)

            turn_norm(0)
            for m in range(GROUPS * B):
                g, b = (GROUPS - 1, m) if m < B else ((m - B) // B, m % B)
                if m < B:
                    pe.wait_ge(h_t_done, b + 1)
                else:
                    pe.wait_ge(mid_done, m - 3)
                te.matmul(bank[2 + m % 4][:], w_in_t[:, g * D:(g + 1) * D], h_t[:, b], start=True,
                          stop=True).then_inc(proj_mm, 1)
            pe.wait_ge(wave_done, 1)
            pe.wait_ge(zero_done, 1)
            pe.wait_ge(ga_done, 1)
            for j in range(NJ):
                last = te.matmul(bank[6 + j // 2][:, (j % 2) * 256:(j % 2 + 1) * 256], wave[:, j * P:(j + 1) * P], w2a[:],
                                 start=True, stop=True)
                if j % 2:
                    last.then_inc(h_mm, 1)
            pe.wait_ge(h_lo_done, 1)
            pe.wait_ge(dft_lo_done, 2)
            for kt in range(NJ):
                if kt >= 2:
                    pe.wait_ge(hs_used, kt - 1)
                for part in range(2):
                    for j in range(NJ):
                        last = three(bank[6 + kt % 2][:, part * 256:(part + 1) * 256],
                                     halves(dft_hi, dft_lo, slice(None), part, j, slice(kt * P, (kt + 1) * P)),
                                     (h_hi[:, j], h_lo[:, j]), j == 0, j == NJ - 1)
                last.then_inc(hs_mm, 1)
            pe.wait_ge(hs_used, NJ)
            pe.wait_ge(gates_done, ORDER * B)
            with pe.Fori(0, ORDER) as n:
                for b in range(B):
                    pe.wait_ge(v_done, 4 * n + b + 1)
                    if b >= 2:
                        pe.wait_ge(tok_lo_done, 4 * n + b - 1)
                    for j in range(NJ):
                        last = te.transpose(bank[b % 2][:, j * P:(j + 1) * P], v[:, b, j * P:(j + 1) * P], ident[:])
                    last.then_inc(v_t, 1)
                pe.wait_ge(tok_lo_done, 4 * n + 4)
                for kt in range(NJ):
                    if kt >= 2:
                        pe.wait_ge(y_done, 8 * n + 2 * kt - 2)
                    for part in range(2):
                        for j in range(NJ):
                            last = three(bank[2 + 2 * (kt % 2) + part][:],
                                         halves(dft_hi, dft_lo, slice(None), part, j, slice(kt * P, (kt + 1) * P)),
                                         halves(tok_hi, tok_lo, slice(None), j), j == 0, j == NJ - 1)
                        last.then_inc(spec_mm, 1)
                for b in range(B):
                    if b >= 2:
                        pe.wait_ge(v_done, 4 * n + B + b - 1)
                    for kt in range(NJ):
                        for part in range(2):
                            if b == 0:
                                pe.wait_ge(y_lo_done, 8 * n + 2 * kt + part + 1)
                            last = three(bank[6 + b % 2][:], halves(y_hi, y_lo, slice(None), part, kt, slice(b * D, (b + 1) * D)),
                                         halves(dft_hi, dft_lo, slice(None), part, kt), kt + part == 0,
                                         kt + part == NJ)
                    last.then_inc(inv_mm, 1)
            pe.wait_ge(ga_done, 1)
            for b in range(B):
                pe.wait_ge(v_done, ORDER * B + b + 1)
                for j in range(NJ):
                    last = te.matmul(bank[2 + b][:, j * D:(j + 1) * D], v[:, b, j * P:(j + 1) * P], w_out_g[:, b],
                                     start=True, stop=True)
                last.then_inc(attn_mm, 1)
            turn_norm(1)
            pe.wait_ge(late_in, 16)
            for b in range(B):
                pe.wait_ge(h2_done, b + 1)
                for j in range(NJ):
                    t = b * NJ + j
                    last = te.matmul(bank[2][:, t * E:(t + 1) * E], h2[:, b, j * P:(j + 1) * P], gate_w_t[:],
                                     start=True, stop=True)
            last.then_inc(logits_mm, 1)
            pe.wait_ge(comb_done, 1)
            for b in range(B):
                if b >= 2:
                    pe.wait_ge(comb_t_done, b - 1)
                for j in range(NJ):
                    last = te.transpose(bank[4 + b % 2][0:2 * E, j * P:(j + 1) * P],
                                        comb[:, b * NJ + j].rearrange("p a e -> p (a e)").bitcast(F32), ident[:])
                last.then_inc(comb_tr, 1)
            pe.wait_ge(comb_t_done, B)
            pe.wait_ge(h2_lo_done, B)
            pe.wait_ge(w_lo_done, n_chunks)
            pe.wait_ge(pick_done, 1)
            LAG = 2
            te.sem_inc(down_mm, READY)
            te.sem_inc(moe_tr, READY)
            with pe.Fori(0, B) as b:
                tokens = (h2_hi[:, bass.ds(b, 1)].rearrange("p o l -> p (o l)"),
                          h2_lo[:, bass.ds(b, 1)].rearrange("p o l -> p (o l)"))
                for u in range(NU + LAG):
                    if u < NU:
                        if u == 0:
                            pe.wait_ge(act_done, READY + NU * b)
                        if u >= 2:
                            pe.wait_ge(silu_done, NU * b + u - 1)
                        three(bank[u % 2][:], halves(w_hi, w_lo, slice(None), u, 0), tokens, True, True).then_inc(gate_mm, 1)
                        if u >= 2:
                            pe.wait_ge(act_done, READY + NU * b + u - 1)
                            pe.wait_ge(gated_done, PAIRS * b + u - 1)
                        three(bank[2 + u % 2][:], halves(w_hi, w_lo, slice(None), u, 1), tokens, True, True).then_inc(up_mm, 1)
                    if u < PAIRS:
                        te.matmul(bank[4 + u % 2][:], pick[:, u],
                                  comb_t[:, bass.ds(b * L, L)], start=True, stop=True).then_inc(weight_mm, 1)
                    if u >= LAG:
                        d = u - LAG
                        if d == 0:
                            pe.wait_ge(moe_done, READY + b)
                        pe.wait_ge(act_lo_done, READY + NU * b + d + 1)
                        three(bank[6][:], halves(w_hi, w_lo, slice(None), d, 2), (act_hi[:, d % 3], act_lo[:, d % 3]),
                              d == 0, d == NU - 1).then_inc(down_mm, 1)
                pe.wait_ge(moe_done, READY + b + 1)
                pe.wait_ge(out_done, READY + b)
                for j in range(NJ):
                    last = te.transpose(bank[7][:, j * P:(j + 1) * P], moe_t[:, j * P:(j + 1) * P], ident[:])
                last.then_inc(moe_tr, 1)


def kernel(**inputs):
    import numpy as _np
    import concourse.bacc as _bacc
    from concourse import mybir as _mybir
    from concourse.bass_utils import run_bass_kernel_spmd as _run

    g = {k.replace("L0_", ""): _np.asarray(a) for k, a in inputs.items()}
    f = _np.float32
    t = (_np.arange(L, dtype=f) / f(L - 1)).astype(f)
    pos = _np.sin(((t[:, None] * _np.arange(EMB, dtype=f)[None]) * f(FREQ)).astype(_np.float64))
    k = _np.arange(L)
    angle = _np.pi * ((2 * k[:, None] + 1) * (2 * k[None] + 1) % (8 * L)) / (4 * L)
    dft = _np.stack([_np.cos(angle), _np.sin(angle)]).reshape(2, NJ, P, L).transpose(2, 0, 1, 3)
    phi = (_np.pi * (2 * k + 1) / (4 * L)).reshape(NJ, P).T
    consts = _np.concatenate([-t.reshape(NJ, P).T] + [a / L ** 2 for a in (_np.cos(phi), _np.sin(phi), -_np.sin(phi))], 1)
    by_group = lambda a: a.reshape(GROUPS, D).T
    cols = _np.concatenate([by_group(g["attn_b_in"])] + [by_group(g["attn_conv_w"][:, i]) for i in range(3)]
                           + [by_group(g["attn_conv_b"])], 1)
    gu = g["ffn_experts_gate_up"].reshape(PAIRS, 2, 2, INTER, D).transpose(4, 0, 2, 1, 3).reshape(D, PAIRS, 2, D)
    dn = g["ffn_experts_down"].reshape(PAIRS, 2, D, INTER).transpose(1, 3, 0, 2).reshape(D, PAIRS, 1, D)
    shared = _np.stack([g["ffn_shared_gate_w"].T, g["ffn_shared_up_w"].T, g["ffn_shared_down_w"].T], 1)
    arrays = {
        "x": g["attn_u"], "c_t": g["c"].T, "wmod": g["wmod"],
        "w1a": _np.concatenate([g["attn_w1"].T, g["attn_b1"][None]]),
        "pos_t": _np.concatenate([pos.T.astype(f), _np.ones((1, L), f)]),
        "w2a": _np.concatenate([g["attn_w2"].T, g["attn_b2"][None]]),
        "ident": _np.eye(P, dtype=f), "w_in_t": g["attn_w_in"].T, "cols": cols,
        "rows": _np.concatenate([g["attn_filt_decay"].ravel(), g["attn_filt_bias"].ravel(), g["attn_b_out"],
                                 g["ffn_e_score_correction_bias"]]),
        "consts": consts.astype(f), "dft": dft.astype(f), "w_out_t": g["attn_w_out"].T,
        "gate_w_t": g["ffn_gate_weight"].T, "pick": _np.tile(_np.repeat(_np.eye(E, dtype=f), INTER, 1), (2, 1)).reshape(2 * E, PAIRS, P),
        "w_experts": _np.concatenate([_np.concatenate([gu, dn], 2), shared[:, None]], 1),
    }
    nc = _bacc.Bacc("TRN2", target_bir_lowering=False, num_devices=1)
    args, feed = {}, {}
    for name, a in arrays.items():
        feed[f"in_{name}"] = _np.ascontiguousarray(a)
        args[name] = nc.dram_tensor(f"in_{name}", a.shape, _mybir.dt.from_np(a.dtype), kind="ExternalInput").ap()
    out = nc.dram_tensor("out_0", (B, L, D), _mybir.dt.float32, kind="ExternalOutput").ap()
    build(nc, args, out)
    r = _run(nc, [feed], core_ids=[0])
    return r.results[0]["out_0"]
```

```python
from contextlib import ExitStack

import concourse.bass as bass
import numpy as np
from concourse import mybir

F32 = mybir.dt.float32
F32R = mybir.dt.float32r
U32 = mybir.dt.uint32
I32 = mybir.dt.int32
ALU = mybir.AluOpType
ACT = mybir.ActivationFunctionType
AX_X = mybir.AxisListType.X

P = 128
B, L, D = 4, 512, 128
NJ = L // P
NT = B * NJ
NK = NJ // 2
LH = L // 2
HB = B // 2
HW = HB * D
STEPS = 4
SLOTS = 3
ORDER = 2
GROUPS = ORDER + 1
EMB, HID = 33, 64
E, TOP_K, N_GROUP, TOPK_GROUP = 32, 6, 8, 4
GS = E // N_GROUP
ROUTED_SCALE = 2.5
INTER = 64
PAIRS = E // 2
NU = PAIRS + 1
EPS = 1e-5
MAX8 = 8
BIG = 3.0e38
FREQ = 10.0
ROUND = 1.5 * 2.0 ** 23
ROOT_BITS = float(0x5F3759DF)
TWO_PI = (6.28125, 1.9340515136718750e-03, 1.2556659146298881e-06)
PI = 3.1415925
USLOTS = 3
HSLOTS = 5
WSLOTS = 4
LAG = 3
STATS_AT, SCALE_AT = ((0, 0), (0, 1)), (0, 2)
NORMED_AT = ((0, 3), (0, 5))
TURNED_AT = ((0, 6), (0, 9))
SCALED_AT = ((0, 6), (0, 9))
LOGITS_AT = ((0, 8), (0, 11))
LOGITS_COPIED_AT = ((0, 8), (0, 11))
ROUTE_AT = ((0, 6), (1, 1), (1, 8))
WEIGHTS_TURNED_AT = ((0, 13), (1, 7), (1, 14))
WEIGHTS_COPIED_AT = ((0, 13), (1, 7), (1, 14))
LATE_CHUNKS_AT = ((0, 1), (0, 2), (0, 4))
EARLY_CHUNKS = 2
CHUNK = 2


def build(nc, io, out):
    ctx = ExitStack()
    with ctx:
        def sem(name):
            return ctx.enter_context(nc.semaphore(name))

        def sb(name, shape, dt=F32):
            return ctx.enter_context(nc.sbuf_tensor(name, shape, dt))

        def overlay(region, *groups):
            got, most = {}, 0
            for group in groups:
                with ExitStack() as inner:
                    words = 0
                    for name, shape, dt in group:
                        got[name] = inner.enter_context(nc.sbuf_tensor(name, shape, dt))
                        words += int(np.prod(shape[1:]))
                    most = max(most, words)
            sb(region, [P, most + 16])
            return got

        GATE_BANKS, UP_BANKS = (0, 1, 4), (2, 3, 5)
        FILTER_ODD, FILTER_EVEN = (7, 1), (6, 0)
        bank = [ctx.enter_context(nc.psum_tensor(f"bank{i}", [P, 512], F32)) for i in range(8)]

        x = sb("x", [P, B, NJ, D])
        fwd_hi = sb("fwd_hi", [P, 2, NK, 2, LH], F32R)
        fwd_lo = sb("fwd_lo", [P, 2, NK, 2, LH], F32R)
        inv_hi = sb("inv_hi", [P, 2, NK, 2, LH], F32R)
        inv_lo = sb("inv_lo", [P, 2, NK, 2, LH], F32R)
        weights = overlay(
            "region_weights",
            [("w_hi", [P, NU, 3, D], F32R), ("w_lo", [P, NU, 3, D], F32R)],
            [("not_used", [P, 2 * NU * 3 * D - ORDER * B * (L + 2)], F32), ("gate_pad", [P, ORDER * B, L + 2], F32)],
        )
        w_hi, w_lo, gate_pad = (weights[k] for k in ("w_hi", "w_lo", "gate_pad"))
        v = sb("v", [P, B, L])
        tok_hi = sb("tok_hi", [P, NJ, B, D], F32R)
        tok_lo = sb("tok_lo", [P, NJ, B, D], F32R)
        w_stage = sb("w_stage", [P, 2, CHUNK, 3, D])
        ident = sb("ident", [P, P])
        w_in_t = sb("w_in_t", [P, GROUPS * D])
        w_out_t = sb("w_out_t", [P, D])
        w_out_g = sb("w_out_g", [P, B, D])
        gate_w_t = sb("gate_w_t", [P, E])
        cols = sb("cols", [P, 15])
        conv_bias = sb("conv_bias", [P, GROUPS])
        consts = sb("consts", [P, 16])
        rows = sb("rows", [P, 672])
        modT = sb("modT", [P, 6, B])
        stats = sb("stats", [P, NT, 6])
        mv = sb("mv", [P, NT, 2])
        var_eps = sb("var_eps", [P, NT])
        bias_col = sb("bias_col", [P, NT])
        rstd = sb("rstd", [P, NT])
        newton = sb("newton", [P, NT])
        c_t = sb("c_t", [P, B])
        silu_c = sb("silu_c", [P, B])
        sign = sb("sign", [P, B])

        big = overlay(
            "region_spectra",
            [("h_t", [P, B, L], F32), ("decay", [P, NJ, ORDER * D], F32),
             ("wmod", [P, 6 * D], F32)],
            [("y_hi", [P, SLOTS, 2, 2 * HW], F32R), ("y_lo", [P, SLOTS, 2, 2 * HW], F32R), ("gap", [P, 16], F32),
             ("odd", [P, 2 * HW], F32), ("folded", [P, 2, 2 * HW], F32)],
            [("silu_g", [P, USLOTS, L], F32), ("act", [P, USLOTS, L], F32),
             ("act_hi", [P, HSLOTS, L], F32R), ("act_lo", [P, HSLOTS, L], F32R), ("moe_t", [P, L], F32)],
        )
        mid = overlay(
            "region_gates",
            [("gates", [P, ORDER, B, L], F32)],
            [("xhat", [P, NT, D], F32), ("comb_t", [E, NT * P], F32)],
        )
        gates, xhat, comb_t = (mid[k] for k in ("gates", "xhat", "comb_t"))
        small = overlay(
            "region_products",
            [("padded", [P, 2, L + 2], F32), ("silu_rep", [P, B, P], F32), ("ga", [P, B, D], F32),
             ("ga_sign", [P, B, D], F32), ("turns", [HID, L], F32), ("angle", [HID, L], F32)],
            [("y", [P, NK, 2, 2 * HW], F32), ("cross", [P, 2, 2 * HW], F32), ("even_odd", [P, 2, 2 * HW], F32)],
            [("scores", [P, NT, E], F32), ("biased", [P, NT, E], F32), ("group_max", [P, NT, N_GROUP + TOPK_GROUP], F32),
             ("group_left", [P, NT, N_GROUP + TOPK_GROUP], F32), ("group_in", [P, NT, N_GROUP], F32),
             ("masked", [P, NT, E + 2], F32), ("left", [P, NT, E + 2], F32), ("top8", [P, NT, MAX8], F32),
             ("weight_sum", [P, NT], F32), ("comb", [P, NT, E], F32)],
        )
        filt = overlay(
            "region_filter",
            [("pos_t", [EMB + 1, L], F32), ("w1a", [EMB + 1, HID], F32), ("w2a", [HID + 1, ORDER * D], F32),
             ("wave", [HID + 1, L], F32)],
            [("filt_c", [P, ORDER, NJ, D], F32), ("filt_s", [P, ORDER, NJ, D], F32)],
            [("pair_weights", [P, WSLOTS, L], F32)],
        )
        filt_c, filt_s, pair_weights = filt["filt_c"], filt["filt_s"], filt["pair_weights"]
        h_t, decay, wmod, y_hi, y_lo, odd, folded = (
            big[k] for k in ("h_t", "decay", "wmod", "y_hi", "y_lo", "odd", "folded"))
        silu_g, act, act_hi, act_lo = (big[k] for k in ("silu_g", "act", "act_hi", "act_lo"))
        moe_t = big["moe_t"]
        padded, silu_rep, ga, ga_sign, turns, angle = (
            small[k] for k in ("padded", "silu_rep", "ga", "ga_sign", "turns", "angle"))
        y, cross, even_odd = small["y"], small["cross"], small["even_odd"]
        scores, biased, group_max, group_left, group_in = (
            small[k] for k in ("scores", "biased", "group_max", "group_left", "group_in"))
        masked, left, top8, weight_sum, comb = (small[k] for k in ("masked", "left", "top8", "weight_sum", "comb"))
        pos_t, w1a, w2a, wave = (filt[k] for k in ("pos_t", "w1a", "w2a", "wave"))

        h_hi = tok_hi[:].rearrange("p j b d -> p (j b d)")[:, 0:NJ * ORDER * D].rearrange("p (j c) -> p j c", j=NJ)
        h_lo = tok_lo[:].rearrange("p j b d -> p (j b d)")[:, 0:NJ * ORDER * D].rearrange("p (j c) -> p j c", j=NJ)
        h_time = decay
        x_tiles = x[:].rearrange("p b j d -> p (b j) d")
        h2 = v
        h2_hi = tok_hi[:].rearrange("p j b d -> p (j b d)").rearrange("p (b l) -> p b l", b=B)
        h2_lo = tok_lo[:].rearrange("p j b d -> p (j b d)").rearrange("p (b l) -> p b l", b=B)
        SA, CA, GA, SB, CB, GB = range(6)
        DECAY, FBIAS, BOUT, CORR = slice(0, 256), slice(256, 512), slice(512, 640), slice(640, 672)

        mod_in, filt_in, const_in, proj_in, late_in = (
            sem(n) for n in ("mod_in", "filt_in", "const_in", "proj_in", "late_in"))
        pair_in = [sem(f"pair_in{i}") for i in range(WSLOTS)]
        x_in = [sem(f"x_in{b}") for b in range(B)]
        c_in, dft_in, inv_in, conv_bias_done = sem("c_in"), sem("dft_in"), sem("inv_in"), sem("conv_bias_done")
        n_chunks = -(-NU // CHUNK)
        w_in_sem = [sem(f"w_in{i}") for i in range(2)]
        silu_c_done, rep_done, mod_mm, ga_mm, ga_copied, mod_done, ga_done, zero_done = (
            sem(n) for n in ("silu_c_done", "rep_done", "mod_mm", "ga_mm", "ga_copied", "mod_done", "ga_done", "zero_done"))
        rstd_done, xhat_done, xhat_t, h_t_done = (
            sem(n) for n in ("rstd_done", "xhat_done", "xhat_t", "h_t_done"))
        proj_mm, padded_done, mid_done, gates_done, v_done = (
            sem(n) for n in ("proj_mm", "padded_done", "mid_done", "gates_done", "v_done"))
        z_mm, angle_in, angle_done, wave_done, decay_done, h_mm, h_done, h_hi_done, h_lo_done, filt_done = (
            sem(n) for n in ("z_mm", "angle_in", "angle_done", "wave_done", "decay_done", "h_mm", "h_done",
                             "h_hi_done", "h_lo_done", "filt_done"))
        w_hi_done, w_lo_done = sem("w_hi_done"), sem("w_lo_done")
        v_t, tok_hi_done, tok_lo_done, odd_mm, even_mm, odd_copied, folded_done, prod_done = (
            sem(n) for n in ("v_t", "tok_hi_done", "tok_lo_done", "odd_mm", "even_mm", "odd_copied", "folded_done",
                             "prod_done"))
        y_done, even_odd_done, y_hi_done, y_lo_done, inv_mm, residual_done = (
            sem(n) for n in ("y_done", "even_odd_done", "y_hi_done", "y_lo_done", "inv_mm", "residual_done"))
        logits_copied, tables_done = sem("logits_copied"), sem("tables_done")
        attn_mm, x1_done, h2_done, h2_hi_done, h2_lo_done, logits_mm, scores_done, comb_done, comb_tr, comb_t_done = (
            sem(n) for n in ("attn_mm", "x1_done", "h2_done", "h2_hi_done", "h2_lo_done", "logits_mm", "scores_done",
                             "comb_done", "comb_tr", "comb_t_done"))
        gate_mm, up_mm, down_mm, silu_done, gated_done, act_done, act_hi_done, act_lo_done = (
            sem(n) for n in ("gate_mm", "up_mm", "down_mm", "silu_done", "gated_done", "act_done",
                             "act_hi_done", "act_lo_done"))
        moe_done, moe_tr, out_done, stored = (sem(n) for n in ("moe_done", "moe_tr", "out_done", "stored"))
        dve_chain, act_chain, pool_chain = sem("dve_chain"), sem("act_chain"), sem("pool_chain")

        block = ctx.enter_context(nc.Block())

        def chunk_units(q):
            return q * CHUNK, min(NU, (q + 1) * CHUNK)

        def unit(b, u):
            return NU * b + u + 1

        def before(u):
            return u - USLOTS if u >= USLOTS else max(r for r in range(NU) if r % USLOTS == u % USLOTS) - NU

        def half_slot(u):
            return HSLOTS - 1 if u == PAIRS else u % (HSLOTS - 1)

        def half_before(u):
            return max(r for r in range(-NU, u) if half_slot(r % NU) == half_slot(u))

        def conv_place(m):
            return (GROUPS - 1, m, padded[:, m % 2]) if m < B else ((m - B) // B, m % B, gate_pad[:, m - B])

        def conv_out(m):
            return v[:, m] if m < B else gates[:, (m - B) // B, m % B]

        def step_batches(s):
            return range(HB * (s % 2), HB * (s % 2) + HB)

        def slot(s, kt):
            return (NK * s + kt) % SLOTS

        def slot_reader(s, kt):
            q = NK * s + kt - SLOTS
            return q // NK if q >= 0 else None

        @block.sync
        def _(sp):
            def load_x(b):
                sp.dma_start(x[:, b], io["x"][b].rearrange("(j p) d -> p j d", p=P)).then_inc(x_in[b], 16)

            sp.dma_start(c_t[:], io["c_t"]).then_inc(c_in, 16)
            load_x(0)
            sp.dma_start(wmod[:], io["wmod"]).then_inc(mod_in, 16)
            load_x(1)
            sp.dma_start(w1a[:], io["w1a"]).then_inc(filt_in, 16)
            sp.dma_start(pos_t[:], io["pos_t"]).then_inc(filt_in, 16)
            load_x(2)
            load_x(3)
            sp.dma_start(cols[:], io["cols"]).then_inc(proj_in, 16)
            sp.dma_start(ident[:], io["ident"]).then_inc(proj_in, 16)
            sp.dma_start(w_in_t[:], io["w_in_t"]).then_inc(proj_in, 16)
            sp.dma_start(w_out_t[:], io["w_out_t"]).then_inc(proj_in, 16)
            sp.dma_start(w2a[:], io["w2a"]).then_inc(filt_in, 16)
            sp.dma_start(rows[:], io["rows"].rearrange("(a n) -> a n", a=1).to_broadcast([P, 672])).then_inc(const_in, 16)
            sp.dma_start(consts[:], io["consts"]).then_inc(const_in, 16)
            sp.dma_start(gate_w_t[:], io["gate_w_t"]).then_inc(late_in, 16)

            def load_weights(q):
                a, z = chunk_units(q)
                if q >= 2:
                    sp.wait_ge(w_lo_done, q - 1)
                sp.dma_start(w_stage[:, q % 2, 0:z - a], io["w_experts"][:, a:z]).then_inc(w_in_sem[q % 2], 16)

            for q in range(n_chunks - 1):
                load_weights(q)
            sp.wait_ge(prod_done, NK * STEPS)

            def store(b):
                sp.wait_ge(out_done, b)
                sp.dma_start(out[bass.ds(b - 1, 1)].rearrange("o (j p) d -> p (o j) d", p=P),
                             x[:, bass.ds(b - 1, 1)].rearrange("p o j d -> p (o j) d")).then_inc(stored, 16)

            def spread_weights(b, first):
                for u in range(PAIRS):
                    if not first or u >= WSLOTS:
                        sp.wait_ge(act_done, unit(b, u - WSLOTS if u >= WSLOTS else u - WSLOTS + PAIRS - NU))
                    for i in range(2):
                        e = 2 * u + i
                        sp.dma_start(pair_weights[i * INTER:(i + 1) * INTER, u % WSLOTS],
                                     comb_t[e:e + 1, bass.ds(b * L, L)].unsqueeze(1).to_broadcast([1, INTER, L])
                                     ).then_inc(pair_in[u % WSLOTS], 16)
                    if u == WSLOTS - 1 and first:
                        load_weights(n_chunks - 1)
                    if u == PAIRS // 2 and not first:
                        store(b)

            sp.wait_ge(comb_t_done, 1)
            spread_weights(0, True)
            sp.wait_ge(comb_t_done, 2)
            spread_weights(1, False)
            sp.wait_ge(comb_t_done, B)
            with sp.Fori(2, B) as b:
                spread_weights(b, False)
            store(B)
            sp.wait_ge(stored, 16 * B)

        @block.gpsimd
        def _(pool):
            chain = [0]

            def link(ins):
                chain[0] += 1
                ins.then_inc(pool_chain, 1)
                pool.wait_ge(pool_chain, chain[0])

            link(nc.gpsimd.memset(padded[:, :, 0:L + 2:L + 1], 0.0))
            link(nc.gpsimd.memset(gate_pad[:, :, 0:L + 2:L + 1], 0.0))
            nc.gpsimd.memset(wave[HID:HID + 1], 1.0).then_inc(zero_done, 1)
            pool.wait_ge(zero_done, 1)
            te = nc.gpsimd
            pool.wait_ge(x_in[B - 1], 16)
            pool.dma_start(fwd_hi[:], io["fwd_hi"].bitcast(F32R)).then_inc(dft_in, 16)
            pool.dma_start(fwd_lo[:], io["fwd_lo"].bitcast(F32R)).then_inc(dft_in, 16)
            pool.dma_start(inv_hi[:], io["inv_hi"].bitcast(F32R)).then_inc(inv_in, 16)
            pool.dma_start(inv_lo[:], io["inv_lo"].bitcast(F32R)).then_inc(inv_in, 16)
            pool.wait_ge(ga_copied, 1)
            link(te.tensor_scalar(ga_sign[:], ga[:], 0.0, 2.0, ALU.is_ge, ALU.mult))
            link(te.tensor_scalar(ga_sign[:], ga_sign[:], -1.0, None, ALU.add))
            link(te.tensor_tensor(ga[:], ga[:], ga_sign[:], ALU.mult))
            link(te.tensor_scalar(ga[:], ga[:], 0.25, None, ALU.max))
            link(te.tensor_tensor(ga[:], ga[:], ga_sign[:], ALU.mult))
            pool.wait_ge(proj_in, 64)
            link(te.tensor_tensor(w_out_g[:], ga[:], w_out_t[:].unsqueeze(1).to_broadcast([P, B, D]), ALU.mult))
            pool.wait_ge(const_in, 32)
            link(te.tensor_tensor(ga[:], ga[:], rows[:, BOUT].unsqueeze(1).to_broadcast([P, B, D]), ALU.mult))
            for b in range(B):
                pool.wait_ge(xhat_done, b + 1)
                te.tensor_tensor(x[:, b], x[:, b], ga[:, b].unsqueeze(1).to_broadcast([P, NJ, D]),
                                 ALU.add).then_inc(ga_done, 1)

            def split_weights(q):
                a, z = chunk_units(q)
                pool.wait_ge(w_hi_done, q + 1)
                if z * 3 * D > 2 * NU * 3 * D - ORDER * B * (L + 2) - NU * 3 * D:
                    pool.wait_ge(gates_done, ORDER * B)
                te.tensor_tensor(w_lo[:, a:z], w_stage[:, q % 2, 0:z - a], w_hi[:, a:z].bitcast(F32),
                                 ALU.subtract).then_inc(w_lo_done, 1)

            def split_h2(b):
                pool.wait_ge(h2_hi_done, b + 1)
                te.tensor_tensor(h2_lo[:, b], h2[:, b], h2_hi[:, b].bitcast(F32),
                                 ALU.subtract).then_inc(h2_lo_done, 1)

            for q in range(EARLY_CHUNKS):
                split_weights(q)
            for s in range(STEPS):
                for kt in range(NK):
                    q = NK * s + kt
                    pool.wait_ge(y_done, q + 1)
                    if q:
                        pool.wait_ge(y_lo_done, 2 * q)
                    te.tensor_tensor(even_odd[:, 0], y[:, kt, 0], y[:, kt, 1], ALU.add).then_inc(even_odd_done, 1)
                    te.tensor_tensor(even_odd[:, 1], y[:, kt, 0], y[:, kt, 1], ALU.subtract).then_inc(even_odd_done, 1)
                    for par in range(2):
                        pool.wait_ge(even_odd_done, 2 * q + par + 1)
                        pool.wait_ge(y_hi_done, 2 * q + par + 1)
                        te.tensor_tensor(y_lo[:, slot(s, kt), par], even_odd[:, par],
                                         y_hi[:, slot(s, kt), par].bitcast(F32), ALU.subtract).then_inc(y_lo_done, 1)
                if 1 <= s < STEPS - 1:
                    split_weights(EARLY_CHUNKS + s - 1)
            pool.wait_ge(y_lo_done, 2 * NK * STEPS)
            link(te.memset(group_max[:], BIG))
            link(te.memset(masked[:, :, 0:E], 0.0))
            te.memset(masked[:, :, E:E + 2], BIG).then_inc(tables_done, 1)
            for q in range(EARLY_CHUNKS + 2, n_chunks - len(LATE_CHUNKS_AT)):
                split_weights(q)
            for b in range(HB):
                split_h2(b)
            def experts(b):
                for u in range(NU):
                    pool.wait_ge(act_hi_done, unit(b, u))
                    nc.gpsimd.tensor_tensor(act_lo[:, half_slot(u)], act[:, u % USLOTS], act_hi[:, half_slot(u)].bitcast(F32),
                                            ALU.subtract).then_inc(act_lo_done, 1)
                    if isinstance(b, int) and (b, u) in LATE_CHUNKS_AT:
                        split_weights(n_chunks - len(LATE_CHUNKS_AT) + LATE_CHUNKS_AT.index((b, u)))
                    if isinstance(b, int) and (b, u) in SCALED_AT:
                        split_h2(HB + SCALED_AT.index((b, u)))

            experts(0)
            with pool.Fori(1, B) as b:
                experts(b)

        @block.scalar
        def _(act_e):
            sc = nc.scalar
            act_e.wait_ge(c_in, 16)
            sc.activation(silu_c[:], c_t[:], ACT.Silu).then_inc(silu_c_done, 1)
            act_e.wait_ge(z_mm, 1)
            sc.activation(angle[:], bank[6][0:HID, :], ACT.Copy, scale=FREQ).then_inc(angle_in, 1)
            act_e.wait_ge(ga_mm, 1)
            sc.activation(ga[:].rearrange("p b d -> p (b d)"), bank[7][:], ACT.Copy).then_inc(ga_copied, 1)
            act_e.wait_ge(const_in, 32)
            sc.activation(rows[:, DECAY], rows[:, DECAY], ACT.Exp).then_inc(act_chain, 1)
            act_e.wait_ge(act_chain, 1)
            for j in range(NJ):
                sc.activation(decay[:, j], rows[:, DECAY], ACT.Exp, scale=consts[:, j:j + 1]).then_inc(decay_done, 1)
            act_e.wait_ge(mod_done, 1)
            for b in range(B):
                act_e.wait_ge(xhat_t, b + 1)
                sc.activation(h_t[:, b], bank[b % 2][:], ACT.Identity, bias=modT[:, SA, b:b + 1],
                              scale=modT[:, CA, b:b + 1]).then_inc(h_t_done, 1)
            act_e.wait_ge(angle_done, 1)
            sc.activation(wave[0:HID], angle[:], ACT.Sin).then_inc(wave_done, 1)
            act_e.wait_ge(zero_done, 1)
            act_e.wait_ge(conv_bias_done, 1)

            def project(m):
                g, b, pad = conv_place(m)
                act_e.wait_ge(proj_mm, m + 1)
                if 2 <= m < B:
                    act_e.wait_ge(v_done, m - 1)
                sc.activation(pad[:, 1:L + 1], bank[2 + m % 4][:], ACT.Identity, bias=cols[:, g:g + 1])
                sc.activation(conv_out(m), bank[2 + m % 4][:], ACT.Identity, bias=conv_bias[:, g:g + 1],
                              scale=cols[:, 6 + g:7 + g]).then_inc(mid_done, 1)

            for m in range(2):
                project(m)
            act_e.wait_ge(h_done, 1)
            sc.activation(h_hi, h_time[:], ACT.Copy).then_inc(h_hi_done, 1)
            def split_weights(q):
                a, z = chunk_units(q)
                act_e.wait_ge(w_in_sem[q % 2], 16 * (q // 2 + 1))
                sc.activation(w_hi[:, a:z], w_stage[:, q % 2, 0:z - a], ACT.Copy).then_inc(w_hi_done, 1)

            def copy_odd(q, bank_odd):
                act_e.wait_ge(odd_mm, q + 1)
                if q:
                    act_e.wait_ge(folded_done, 2 * q)
                sc.activation(odd[:], bank_odd[:], ACT.Copy).then_inc(odd_copied, 1)

            def split_tokens(s, b):
                act_e.wait_ge(v_t, HB * s + b % HB + 1)
                sc.activation(tok_hi[:, :, b], bank[b % 2][:].rearrange("p (j d) -> p j d", j=NJ),
                              ACT.Copy).then_inc(tok_hi_done, 1)

            for m in range(2, B):
                project(m)
            for kt in range(NK):
                copy_odd(kt, bank[FILTER_ODD[kt]])
            for q in range(2):
                split_weights(q)
            for m in range(B, 2 * B):
                project(m)
            for b in range(HB):
                split_tokens(0, b)
            for m in range(2 * B, GROUPS * B):
                project(m)
            def split_spectra(q):
                s, kt = divmod(q, NK)
                if slot_reader(s, kt) is not None:
                    act_e.wait_ge(inv_mm, HB * (slot_reader(s, kt) + 1))
                for par in range(2):
                    act_e.wait_ge(even_odd_done, 2 * q + par + 1)
                    sc.activation(y_hi[:, slot(s, kt), par], even_odd[:, par], ACT.Copy).then_inc(y_hi_done, 1)

            for s in range(STEPS):
                if s >= 2:
                    for b in step_batches(s):
                        split_tokens(s, b)
                if s:
                    split_spectra(NK * s - 1)
                copy_odd(NK + NK * s, bank[2])
                if s == 0:
                    for b in step_batches(1):
                        split_tokens(1, b)
                copy_odd(NK + NK * s + 1, bank[4])
                split_spectra(NK * s)
                if s < STEPS - 1:
                    split_weights(2 + s)
            split_spectra(NK * STEPS - 1)
            for q in range(STEPS + 1, n_chunks - len(LATE_CHUNKS_AT)):
                split_weights(q)

            def normalise(b):
                act_e.wait_ge(rstd_done, b + 1)
                for t in range(b * NJ, (b + 1) * NJ):
                    last = sc.activation(xhat[:, t], x_tiles[:, t], ACT.Identity, bias=bias_col[:, t:t + 1],
                                         scale=rstd[:, t:t + 1])
                last.then_inc(xhat_done, 1)

            def scale_by_channel(b):
                act_e.wait_ge(xhat_t, B + b + 1)
                sc.activation(h2[:, b], bank[b if b < HB else 7][:], ACT.Identity, bias=modT[:, SB, b:b + 1],
                              scale=modT[:, CB, b:b + 1]).then_inc(h2_done, 1)
                act_e.wait_ge(h2_done, b + 1)
                sc.activation(h2_hi[:, b], h2[:, b], ACT.Copy).then_inc(h2_hi_done, 1)

            def batch_scores(b):
                return scores[:, b * NJ:(b + 1) * NJ].rearrange("p t e -> p (t e)")

            def logits_out(b):
                act_e.wait_ge(logits_mm, b + 1)
                if b < HB:
                    sc.activation(batch_scores(b), bank[4][:, b * NJ * E:(b + 1) * NJ * E],
                                  ACT.Sigmoid).then_inc(scores_done, 1)
                else:
                    sc.activation(batch_scores(b), bank[7][:, 0:NJ * E], ACT.Copy).then_inc(logits_copied, 1)
                if b == B - 1:
                    act_e.wait_ge(logits_copied, B - HB)
                    late = scores[:, HB * NJ:NT].rearrange("p t e -> p (t e)")
                    sc.activation(late, late, ACT.Sigmoid).then_inc(scores_done, 2)

            def weights_by_expert(b):
                act_e.wait_ge(comb_tr, b + 1)
                sc.activation(comb_t[:, b * L:(b + 1) * L], bank[7 if b else 5][0:E, :],
                              ACT.Copy).then_inc(comb_t_done, 1)

            act_e.wait_ge(y_lo_done, 2 * NK * STEPS)
            normalise(0)
            scale_by_channel(0)
            logits_out(0)
            normalise(1)
            scale_by_channel(1)
            weights_by_expert(0)
            logits_out(1)

            def high(b, d):
                act_e.wait_ge(act_done, unit(b, d))
                u = d % NU
                last_user = half_before(u) + d - u
                if not isinstance(b, int) or NU * b + last_user >= 0:
                    act_e.wait_ge(down_mm, unit(b, last_user))
                sc.activation(act_hi[:, half_slot(u)], act[:, u % USLOTS], ACT.Copy).then_inc(act_hi_done, 1)

            def moe_sum(b):
                act_e.wait_ge(down_mm, unit(b, -1))
                sc.activation(moe_t[:], bank[6][:], ACT.Copy, scale=modT[:, GB, bass.ds(b - 1, 1)]).then_inc(moe_done, 1)

            def experts(b, first):
                for u in range(NU):
                    if u == LAG and not first:
                        moe_sum(b)
                    act_e.wait_ge(gate_mm, unit(b, u))
                    sc.activation(silu_g[:, u % USLOTS], bank[GATE_BANKS[u % USLOTS]][:], ACT.Silu).then_inc(silu_done, 1)
                    if u >= 1 or not first:
                        high(b, u - 1)
                    if isinstance(b, int):
                        if (b, u) in LATE_CHUNKS_AT:
                            split_weights(n_chunks - len(LATE_CHUNKS_AT) + LATE_CHUNKS_AT.index((b, u)))
                        if (b, u) in NORMED_AT:
                            normalise(HB + NORMED_AT.index((b, u)))
                        if (b, u) in SCALED_AT:
                            scale_by_channel(HB + SCALED_AT.index((b, u)))
                        if (b, u) in LOGITS_COPIED_AT:
                            logits_out(HB + LOGITS_COPIED_AT.index((b, u)))
                        if (b, u) in WEIGHTS_COPIED_AT:
                            weights_by_expert(1 + WEIGHTS_COPIED_AT.index((b, u)))

            experts(0, True)
            experts(1, False)
            with act_e.Fori(2, B) as b:
                experts(b, False)
            high(B, -1)
            moe_sum(B)

        @block.vector
        def _(dve):
            ve = nc.vector
            chain = [0]

            def link(ins):
                chain[0] += 1
                ins.then_inc(dve_chain, 1)
                dve.wait_ge(dve_chain, chain[0])

            def tile_stats(b):
                for t in range(b * NJ, (b + 1) * NJ):
                    last = ve.bn_stats(stats[:, t], x_tiles[:, t])
                link(last)
                for t in range(b * NJ, (b + 1) * NJ):
                    last = ve.bn_aggr(mv[:, t], stats[:, t])
                link(last)

            def norm_scale(at):
                link(ve.tensor_scalar(var_eps[:, at], mv[:, at, 1], EPS, None, ALU.add))
                link(ve.tensor_scalar(rstd[:, at].bitcast(I32), var_eps[:, at].bitcast(I32), -0.5, ROOT_BITS,
                                      ALU.mult, ALU.add))
                for step in range(3):
                    link(ve.tensor_tensor(newton[:, at], rstd[:, at], rstd[:, at], ALU.mult))
                    link(ve.scalar_tensor_tensor(newton[:, at], newton[:, at], -0.5, var_eps[:, at], ALU.mult, ALU.mult))
                    last = ve.scalar_tensor_tensor(rstd[:, at], newton[:, at], 1.5, rstd[:, at], ALU.add, ALU.mult)
                    if step < 2:
                        link(last)
                return last

            dve.wait_ge(silu_c_done, 1)
            ve.tensor_copy(silu_rep[:], silu_c[:].unsqueeze(2).to_broadcast([P, B, P])).then_inc(rep_done, 1)
            for b in range(2):
                dve.wait_ge(x_in[b], 16)
                tile_stats(b)
            dve.wait_ge(mod_mm, 1)
            link(ve.tensor_copy(modT[:].rearrange("p m b -> p (m b)"), bank[6][:, 0:6 * B]))
            ve.tensor_scalar(modT[:, CA], modT[:, CA], 1.0, None, ALU.add)
            ve.tensor_scalar(modT[:, CB], modT[:, CB], 1.0, None, ALU.add)
            link(ve.tensor_scalar(sign[:], modT[:, GB], 0.0, 2.0, ALU.is_ge, ALU.mult))
            link(ve.tensor_scalar(sign[:], sign[:], -1.0, None, ALU.add))
            link(ve.tensor_tensor(modT[:, GB], modT[:, GB], sign[:], ALU.mult))
            ve.scalar_tensor_tensor(modT[:, GB], modT[:, GB], 0.25, sign[:], ALU.max, ALU.mult).then_inc(mod_done, 1)
            for b in range(2, B):
                dve.wait_ge(x_in[b], 16)
                tile_stats(b)
            link(norm_scale(slice(0, NT)))
            for b in range(B):
                for t in range(b * NJ, (b + 1) * NJ):
                    last = ve.tensor_scalar(xhat[:, t], x_tiles[:, t], mv[:, t, 0:1], rstd[:, t:t + 1],
                                            ALU.subtract, ALU.mult)
                last.then_inc(xhat_done, 1)
            dve.wait_ge(angle_in, 1)
            link(ve.tensor_scalar(turns[:], angle[:], float(1 / (2 * np.pi)), ROUND, ALU.mult, ALU.add))
            link(ve.tensor_scalar(turns[:], turns[:], -ROUND, None, ALU.add))
            for part in TWO_PI:
                link(ve.scalar_tensor_tensor(angle[:], turns[:], -part, angle[:], ALU.mult, ALU.add))
            ve.tensor_scalar(angle[:], angle[:], PI, -PI, ALU.min, ALU.max).then_inc(angle_done, 1)
            dve.wait_ge(proj_in, 64)
            link(ve.tensor_tensor(conv_bias[:], cols[:, 0:3], cols[:, 6:9], ALU.mult))
            ve.tensor_tensor(conv_bias[:], conv_bias[:], cols[:, 12:15], ALU.add).then_inc(conv_bias_done, 1)
            for j in range(NJ):
                dve.wait_ge(h_mm, j // 2 + 1)
                dve.wait_ge(decay_done, j + 1)
                link(ve.tensor_tensor(h_time[:, j], bank[6 + j // 2][:, (j % 2) * 256:(j % 2 + 1) * 256], decay[:, j],
                                      ALU.mult))
                last = ve.tensor_tensor(h_time[:, j], h_time[:, j], rows[:, FBIAS], ALU.add)
            last.then_inc(h_done, 1)
            dve.wait_ge(h_hi_done, 1)
            ve.tensor_tensor(h_lo, h_time[:], h_hi.bitcast(F32), ALU.subtract).then_inc(h_lo_done, 1)

            def outer_taps(m):
                g, b, pad = conv_place(m)
                dst = conv_out(m)
                dve.wait_ge(mid_done, m + 1)
                link(ve.scalar_tensor_tensor(dst, pad[:, 0:L], cols[:, 3 + g:4 + g], dst, ALU.mult, ALU.add))
                ve.scalar_tensor_tensor(dst, pad[:, 2:L + 2], cols[:, 9 + g:10 + g], dst,
                                        ALU.mult, ALU.add).then_inc(v_done if m < B else gates_done, 1)

            def fold(q, bank_even):
                dve.wait_ge(even_mm, q + 1)
                dve.wait_ge(odd_copied, q + 1)
                ve.tensor_tensor(folded[:, 0], bank_even[:], odd[:], ALU.add).then_inc(folded_done, 1)
                ve.tensor_tensor(folded[:, 1], bank_even[:], odd[:], ALU.subtract).then_inc(folded_done, 1)
                dve.wait_ge(folded_done, 2 * q + 2)

            def rotate(kt):
                two = lambda a: a.rearrange("p (n d) -> p n d", n=ORDER)
                for side in range(2):
                    hc, hs = (two(folded[:, side, i * HW:(i + 1) * HW]) for i in ((0, 1), (1, 0))[side])
                    i = 2 * kt + side
                    cos, sin, neg = (consts[:, 4 * a + i:4 * a + i + 1] for a in (1, 2, 3))
                    ve.tensor_scalar(filt_c[:, :, i], hc, cos, None, ALU.mult)
                    link(ve.tensor_scalar(filt_s[:, :, i], hs, cos, None, ALU.mult))
                    ve.scalar_tensor_tensor(filt_c[:, :, i], hs, sin, filt_c[:, :, i], ALU.mult, ALU.add)
                    ve.scalar_tensor_tensor(filt_s[:, :, i], hc, neg, filt_s[:, :, i], ALU.mult,
                                            ALU.add).then_inc(filt_done, 1)

            def split_tokens(s, b):
                dve.wait_ge(tok_hi_done, HB * s + b % HB + 1)
                ve.tensor_tensor(tok_lo[:, :, b], bank[b % 2][:].rearrange("p (j d) -> p j d", j=NJ),
                                 tok_hi[:, :, b].bitcast(F32), ALU.subtract).then_inc(tok_lo_done, 1)

            def multiply_spectra(s, kt):
                n, q = s // 2, NK * s + kt
                shape = [P, 2, 2 * HB, D]
                tiles = lambda a: a.rearrange("p i (r d) -> p i r d", d=D)
                f = lambda a: a[:, n, 2 * kt:2 * kt + 2].unsqueeze(2).to_broadcast(shape)
                if s:
                    dve.wait_ge(even_odd_done, 2 * (q - NK) + 2)
                ve.tensor_tensor(tiles(y[:, kt]), tiles(folded[:]), f(filt_c), ALU.mult)
                ve.tensor_tensor(tiles(cross[:]), tiles(folded[:]), f(filt_s), ALU.mult).then_inc(prod_done, 1)

            def add_products(s, kt):
                dve.wait_ge(prod_done, NK * s + kt + 1)
                for side in range(2):
                    for i in range(2):
                        dst = y[:, kt, side, i * HW:(i + 1) * HW]
                        last = ve.tensor_tensor(dst, dst, cross[:, side, (1 - i) * HW:(2 - i) * HW],
                                                ALU.subtract if i == side else ALU.add)
                last.then_inc(y_done, 1)

            def gate(s, b):
                by_parity = lambda a: a.rearrange("p (m par) -> p par m", par=2)
                dve.wait_ge(inv_mm, HB * s + b % HB + 1)
                ve.tensor_tensor(by_parity(v[:, b]), bank[6 + b % 2][:].rearrange("p (par m) -> p par m", par=2),
                                 by_parity(gates[:, s // 2, b]), ALU.mult).then_inc(v_done, 1)

            def residual(b):
                dve.wait_ge(attn_mm, b + 1)
                dve.wait_ge(ga_done, b + 1)
                ve.tensor_tensor(x[:, b].rearrange("p j d -> p (j d)"), bank[2 + b % 2][:],
                                 x[:, b].rearrange("p j d -> p (j d)"), ALU.add).then_inc(x1_done, 1)

            def second_norm(b, count):
                at = slice(b * NJ, (b + count) * NJ)
                link(norm_scale(at))
                ve.scalar_tensor_tensor(bias_col[:, at], mv[:, at, 0], -1.0, rstd[:, at],
                                        ALU.mult, ALU.mult).then_inc(rstd_done, count)

            def route_groups(b):
                at = slice(b * NJ, (b + 1) * NJ)
                dve.wait_ge(scores_done, b + 1)
                link(ve.tensor_tensor(biased[:, at], scores[:, at], rows[:, CORR].unsqueeze(1).to_broadcast([P, NJ, E]),
                                      ALU.add))
                link(ve.tensor_reduce(group_max[:, at, 0:N_GROUP], biased[:, at].rearrange("p t (g s) -> p t g s", g=N_GROUP),
                                      AX_X, ALU.max))
                for t in range(b * NJ, (b + 1) * NJ):
                    last = ve.max(top8[:, t], group_max[:, t])
                link(last)
                for t in range(b * NJ, (b + 1) * NJ):
                    last = ve.match_replace(group_left[:, t], top8[:, t], group_max[:, t], -BIG)
                link(last)
                link(ve.tensor_scalar(group_in[:, at], group_left[:, at, 0:N_GROUP], -BIG, None, ALU.is_equal))

            def route_experts(b):
                at = slice(b * NJ, (b + 1) * NJ)
                for s in range(GS):
                    last = ve.copy_predicated(masked[:, at, s:E:GS], group_in[:, at].bitcast(U32), biased[:, at, s:E:GS])
                link(last)
                for t in range(b * NJ, (b + 1) * NJ):
                    last = ve.max(top8[:, t], masked[:, t])
                link(last)
                for t in range(b * NJ, (b + 1) * NJ):
                    last = ve.match_replace(left[:, t], top8[:, t], masked[:, t], -BIG)
                link(last)

            def route_weights(b):
                at = slice(b * NJ, (b + 1) * NJ)
                link(ve.scalar_tensor_tensor(scores[:, at], left[:, at, 0:E], -BIG, scores[:, at], ALU.is_equal, ALU.mult))
                link(ve.tensor_reduce(weight_sum[:, at], scores[:, at], AX_X, ALU.add))
                link(ve.tensor_scalar(weight_sum[:, at], weight_sum[:, at], 1e-20, None, ALU.add))
                link(ve.reciprocal(weight_sum[:, at], weight_sum[:, at]))
                ve.scalar_tensor_tensor(comb[:, at], scores[:, at], ROUTED_SCALE,
                                        weight_sum[:, at].unsqueeze(2).to_broadcast([P, NJ, E]), ALU.mult,
                                        ALU.mult).then_inc(comb_done, 1)

            for m in range(B):
                outer_taps(m)
            for kt in range(NK):
                if kt:
                    dve.wait_ge(filt_done, 2 * kt)
                fold(kt, bank[FILTER_EVEN[kt]])
                rotate(kt)
            for b in range(HB):
                split_tokens(0, b)
            for m in (B, B + 1):
                outer_taps(m)
            dve.wait_ge(filt_done, 2 * NK)
            dve.wait_ge(ga_done, B)
            for s in range(STEPS):
                for kt in range(NK):
                    if NK * s + kt:
                        dve.wait_ge(y_done, NK * s + kt)
                    fold(NK + NK * s + kt, bank[3 + 2 * kt])
                    if s and kt == NK - 1:
                        for b in step_batches(s - 1):
                            gate(s - 1, b)
                    multiply_spectra(s, kt)
                    if s + kt == 0 or (1 <= s < STEPS - 1 and kt == NK - 1):
                        for b in step_batches(s + 1):
                            split_tokens(s + 1, b)
                    add_products(s, kt)
                if s < STEPS - 1:
                    for m in (B + 2 + 2 * s, B + 3 + 2 * s):
                        outer_taps(m)
            for b in range(HB):
                residual(b)
            for b in range(HB):
                dve.wait_ge(x1_done, b + 1)
                tile_stats(b)
                second_norm(b, 1)
            gate(STEPS - 1, HB)
            dve.wait_ge(tables_done, 1)
            route_groups(0)
            route_experts(0)
            route_weights(0)
            gate(STEPS - 1, B - 1)
            for b in range(HB, B):
                residual(b)

            def output(b):
                dve.wait_ge(moe_tr, b)
                done = x[:, bass.ds(b - 1, 1)].rearrange("p o j d -> p (o j d)")
                ve.tensor_tensor(done, bank[7][:], done, ALU.add).then_inc(out_done, 1)

            def experts(b, first):
                for u in range(NU):
                    dve.wait_ge(silu_done, unit(b, u))
                    dve.wait_ge(up_mm, unit(b, u))
                    if not first or u >= USLOTS:
                        dve.wait_ge(act_lo_done, unit(b, before(u)))
                    if u < PAIRS:
                        ve.tensor_tensor(act[:, u % USLOTS], bank[UP_BANKS[u % USLOTS]][:], silu_g[:, u % USLOTS],
                                         ALU.mult).then_inc(gated_done, 1)
                        dve.wait_ge(pair_in[u % WSLOTS], 32 * (PAIRS // WSLOTS * b + u // WSLOTS + 1))
                        dve.wait_ge(gated_done, PAIRS * b + u + 1)
                        ve.tensor_tensor(act[:, u % USLOTS], pair_weights[:, u % WSLOTS], act[:, u % USLOTS],
                                         ALU.mult).then_inc(act_done, 1)
                    else:
                        ve.tensor_tensor(act[:, u % USLOTS], bank[UP_BANKS[u % USLOTS]][:], silu_g[:, u % USLOTS],
                                         ALU.mult).then_inc(act_done, 1)
                    if u == LAG + 2 and not first:
                        output(b)
                    if isinstance(b, int):
                        if (b, u) in STATS_AT:
                            dve.wait_ge(x1_done, HB + STATS_AT.index((b, u)) + 1)
                            tile_stats(HB + STATS_AT.index((b, u)))
                        if (b, u) == SCALE_AT:
                            second_norm(HB, B - HB)
                        for r, (rb, ru) in enumerate(ROUTE_AT):
                            for step, route in enumerate((route_groups, route_experts, route_weights)):
                                if (b, u) == (rb, ru + step):
                                    route(1 + r)

            experts(0, True)
            experts(1, False)
            with dve.Fori(2, B) as b:
                experts(b, False)
            output(B)

        @block.tensor
        def _(pe):
            te = nc.tensor

            def three(dst, stat, mov, start, stop):
                (sh, sl), (mh, ml) = stat, mov
                te.matmul(dst, sl, mh, start=start, stop=False)
                te.matmul(dst, sh, ml, start=False, stop=False)
                return te.matmul(dst, sh, mh, start=False, stop=stop)

            def halves(hi, lo, *at):
                return hi[at], lo[at]

            pe.wait_ge(mod_in, 16)
            pe.wait_ge(silu_c_done, 1)
            for m in range(6):
                last = te.matmul(bank[6][:, m * B:(m + 1) * B], wmod[:, m * D:(m + 1) * D], silu_c[:], start=True, stop=True)
            last.then_inc(mod_mm, 1)
            pe.wait_ge(rep_done, 1)
            for b in range(B):
                last = te.matmul(bank[7][:, b * D:(b + 1) * D], silu_rep[:, b], wmod[:, GA * D:(GA + 1) * D],
                                 start=True, stop=True)
            last.then_inc(ga_mm, 1)
            pe.wait_ge(filt_in, 48)
            pe.wait_ge(mod_done, 1)
            te.matmul(bank[6][0:HID, :], w1a[:], pos_t[:], start=True, stop=True).then_inc(z_mm, 1)
            pe.wait_ge(proj_in, 64)

            def turn_norm(b, norm):
                late = norm and b >= HB
                pe.wait_ge(xhat_done, norm * B + b + 1)
                if not norm and b >= 2:
                    pe.wait_ge(h_t_done, b - 1)
                if late and b > HB:
                    pe.wait_ge(logits_copied, b - HB)
                for j in range(NJ):
                    last = te.transpose(bank[7 if late else b % 2][:, j * P:(j + 1) * P], xhat[:, b * NJ + j], ident[:])
                last.then_inc(xhat_t, 1)

            def project(m):
                g, b, _ = conv_place(m)
                if m < B:
                    pe.wait_ge(h_t_done, b + 1)
                else:
                    pe.wait_ge(mid_done, m - 3)
                te.matmul(bank[2 + m % 4][:], w_in_t[:, g * D:(g + 1) * D], h_t[:, b], start=True,
                          stop=True).then_inc(proj_mm, 1)

            def forward(even, odd_bank, kt, moving):
                for par, dst, done in ((1, odd_bank, odd_mm), (0, even, even_mm)):
                    for part in range(2):
                        for j in range(NK):
                            last = three(dst[:, part * HW:(part + 1) * HW],
                                         halves(fwd_hi, fwd_lo, slice(None), par, j, part, slice(kt * P, (kt + 1) * P)),
                                         moving(par * NK + j), j == 0, j == NK - 1)
                    last.then_inc(done, 1)

            for b in range(B):
                turn_norm(b, 0)
            for m in range(2):
                project(m)
            pe.wait_ge(wave_done, 1)
            pe.wait_ge(zero_done, 1)
            pe.wait_ge(ga_copied, 1)
            for j in range(NJ):
                last = te.matmul(bank[6 + j // 2][:, (j % 2) * 256:(j % 2 + 1) * 256], wave[:, j * P:(j + 1) * P], w2a[:],
                                 start=True, stop=True)
                if j % 2:
                    last.then_inc(h_mm, 1)
            for m in range(2, B):
                project(m)
            pe.wait_ge(h_lo_done, 1)
            pe.wait_ge(dft_in, 32)
            for kt in range(NK):
                forward(bank[FILTER_EVEN[kt]], bank[FILTER_ODD[kt]], kt, lambda t: (h_hi[:, t], h_lo[:, t]))
            for m in range(B, 2 * B):
                project(m)

            def to_tokens(s):
                for b in step_batches(s):
                    pe.wait_ge(v_done, HB * s + b % HB + 1)
                    if s:
                        pe.wait_ge(tok_lo_done, HB * s + b % HB - 1)
                    for j in range(NJ):
                        par, jj = divmod(j, NK)
                        last = te.transpose(bank[b % 2][:, j * P:(j + 1) * P],
                                            v[:, b, 2 * P * jj + par:2 * P * (jj + 1):2], ident[:])
                    last.then_inc(v_t, 1)

            def step_forward(s):
                b = step_batches(s)[0]
                pe.wait_ge(tok_lo_done, HB * (s + 1))
                for kt in range(NK):
                    if s:
                        pe.wait_ge(folded_done, 2 * (NK * s + kt) + 2)
                    else:
                        pe.wait_ge(mid_done, GROUPS * B - 2 + 2 * kt)
                    forward(bank[3 + 2 * kt], bank[2 + 2 * kt], kt, lambda t: (tok_hi[:, t, b:b + HB], tok_lo[:, t, b:b + HB]))

            def back(s, b):
                i = b % HB
                if s:
                    pe.wait_ge(v_done, B + HB * (s - 1) + i + 1)
                for par in range(2):
                    for kt in range(NK):
                        pe.wait_ge(y_lo_done, 2 * (NK * s + kt) + par + 1)
                        for part in range(2):
                            at = slice(part * HW + i * D, part * HW + (i + 1) * D)
                            last = three(bank[6 + i][:, par * LH:(par + 1) * LH],
                                         halves(y_hi, y_lo, slice(None), slot(s, kt), par, at),
                                         halves(inv_hi, inv_lo, slice(None), par, kt, part),
                                         kt + part == 0, kt + part == NK)
                    if par == 0 and (s, b) == (STEPS - 1, HB):
                        turn_norm(0, 1)
                last.then_inc(inv_mm, 1)

            def attention_out(b):
                pe.wait_ge(v_done, (ORDER * B) + b + 1)
                pe.wait_ge(ga_done, b + 1)
                if b >= 2:
                    pe.wait_ge(x1_done, b - 1)
                for j in range(NJ):
                    last = te.matmul(bank[2 + b % 2][:, j * D:(j + 1) * D], v[:, b, j * P:(j + 1) * P], w_out_g[:, b],
                                     start=True, stop=True)
                last.then_inc(attn_mm, 1)

            def logits(b):
                pe.wait_ge(h2_done, b + 1)
                if b == 1:
                    pe.wait_ge(scores_done, b)
                for j in range(NJ):
                    dst = bank[4][:, (b * NJ + j) * E:(b * NJ + j + 1) * E] if b < HB else bank[7][:, j * E:(j + 1) * E]
                    last = te.matmul(dst, h2[:, b, j * P:(j + 1) * P], gate_w_t[:], start=True, stop=True)
                last.then_inc(logits_mm, 1)

            def weights_by_expert(b):
                pe.wait_ge(comb_done, b + 1)
                if b == 1:
                    pe.wait_ge(logits_copied, B - HB)
                if b >= 2:
                    pe.wait_ge(comb_t_done, b)
                    pe.wait_ge(out_done, 1)
                for j in range(NJ):
                    last = te.transpose(bank[7 if b else 5][0:E, j * P:(j + 1) * P], comb[:, b * NJ + j], ident[:])
                last.then_inc(comb_tr, 1)

            pe.wait_ge(folded_done, 2 * NK)
            to_tokens(0)
            for m in range(2 * B, GROUPS * B):
                project(m)
            step_forward(0)
            pe.wait_ge(inv_in, 32)
            for s in range(1, STEPS):
                to_tokens(s)
                step_forward(s)
                for b in step_batches(s - 1):
                    back(s - 1, b)
            for b in range(HB):
                attention_out(b)
            back(STEPS - 1, HB)
            pe.wait_ge(late_in, 16)
            logits(0)
            back(STEPS - 1, HB + 1)
            turn_norm(1, 1)
            attention_out(HB)
            weights_by_expert(0)
            attention_out(B - 1)
            logits(1)
            pe.wait_ge(h2_lo_done, 1)

            def down(b, d):
                u = d % NU
                if u == 0 and (not isinstance(b, int) or b > 0):
                    pe.wait_ge(moe_done, b)
                pe.wait_ge(act_lo_done, unit(b, d))
                three(bank[6][:], halves(w_hi, w_lo, slice(None), u, 2), (act_hi[:, half_slot(u)], act_lo[:, half_slot(u)]),
                      u == 0, u == NU - 1).then_inc(down_mm, 1)

            def turn_sum(b):
                pe.wait_ge(moe_done, b)
                if isinstance(b, int) and b == 1:
                    pe.wait_ge(comb_t_done, 2)
                for j in range(NJ):
                    last = te.transpose(bank[7][:, j * P:(j + 1) * P], moe_t[:, j * P:(j + 1) * P], ident[:])
                last.then_inc(moe_tr, 1)

            def experts(b, first):
                tokens = (h2_hi[:, bass.ds(b, 1)].rearrange("p o l -> p (o l)"),
                          h2_lo[:, bass.ds(b, 1)].rearrange("p o l -> p (o l)"))
                for u in range(NU):
                    if not first or u >= USLOTS:
                        pe.wait_ge(act_done, unit(b, before(u)))
                    if first and u == USLOTS - 1:
                        pe.wait_ge(scores_done, HB)
                        pe.wait_ge(comb_t_done, 1)
                    if first:
                        pe.wait_ge(w_lo_done, u // CHUNK + 1)
                    three(bank[GATE_BANKS[u % USLOTS]][:], halves(w_hi, w_lo, slice(None), u, 0), tokens, True, True).then_inc(gate_mm, 1)
                    if first and u == 0:
                        pe.wait_ge(x1_done, B)
                    three(bank[UP_BANKS[u % USLOTS]][:], halves(w_hi, w_lo, slice(None), u, 1), tokens, True, True).then_inc(up_mm, 1)
                    if not first or u >= LAG:
                        down(b, u - LAG)
                    if u == LAG + 1 and not first:
                        turn_sum(b)
                    if isinstance(b, int):
                        if (b, u) in TURNED_AT:
                            turn_norm(HB + TURNED_AT.index((b, u)), 1)
                        if (b, u) in LOGITS_AT:
                            logits(HB + LOGITS_AT.index((b, u)))
                        if (b, u) in WEIGHTS_TURNED_AT:
                            weights_by_expert(1 + WEIGHTS_TURNED_AT.index((b, u)))

            experts(0, True)
            pe.wait_ge(comb_t_done, 2)
            pe.wait_ge(h2_lo_done, 2)
            experts(1, False)
            pe.wait_ge(comb_t_done, B)
            pe.wait_ge(h2_lo_done, B)
            with pe.Fori(2, B) as b:
                experts(b, False)
            for d in range(-LAG, 0):
                down(B, d)
            turn_sum(B)


def kernel(**inputs):
    import numpy as _np
    import concourse.bacc as _bacc
    from concourse import mybir as _mybir
    from concourse.bass_utils import run_bass_kernel_spmd as _run

    g = {k.replace("L0_", ""): _np.asarray(a) for k, a in inputs.items()}
    f = _np.float32
    t = (_np.arange(L, dtype=f) / f(L - 1)).astype(f)
    pos = _np.sin(((t[:, None] * _np.arange(EMB, dtype=f)[None]) * f(FREQ)).astype(_np.float64))
    half = lambda a: _np.ldexp(_np.round(_np.ldexp(_np.frexp(a)[0], 12)), _np.frexp(a)[1] - 12)
    token = (_np.arange(L).reshape(LH, 2).T).ravel()
    k = _np.arange(LH)
    angle = _np.pi * ((2 * k[:, None] + 1) * (2 * token[None] + 1) % (8 * L)) / (4 * L)
    dft = _np.stack([_np.cos(angle), _np.sin(angle)])
    fwd = dft.reshape(2, LH, 2, NK, P).transpose(4, 2, 3, 0, 1)
    inv = dft.reshape(2, NK, P, 2, LH).transpose(2, 3, 1, 0, 4)
    near = k.reshape(NK, P)
    freq = _np.stack([near, L - 1 - near], 1).reshape(2 * NK, P).T
    phi = _np.pi * (2 * freq + 1) / (4 * L)
    consts = _np.concatenate([-t[token].reshape(NJ, P).T] + [a / L ** 2 for a in (_np.cos(phi), _np.sin(phi), -_np.sin(phi))], 1)
    by_group = lambda a: a.reshape(GROUPS, D).T
    cols = _np.concatenate([by_group(g["attn_b_in"])] + [by_group(g["attn_conv_w"][:, i]) for i in range(3)]
                           + [by_group(g["attn_conv_b"])], 1)
    gu = g["ffn_experts_gate_up"].reshape(PAIRS, 2, 2, INTER, D).transpose(4, 0, 2, 1, 3).reshape(D, PAIRS, 2, D)
    dn = g["ffn_experts_down"].reshape(PAIRS, 2, D, INTER).transpose(1, 3, 0, 2).reshape(D, PAIRS, 1, D)
    shared = _np.stack([g["ffn_shared_gate_w"].T, g["ffn_shared_up_w"].T, g["ffn_shared_down_w"].T], 1)
    arrays = {
        "x": g["attn_u"], "c_t": g["c"].T, "wmod": g["wmod"],
        "w1a": _np.concatenate([g["attn_w1"].T, g["attn_b1"][None]]),
        "pos_t": _np.concatenate([pos[token].T.astype(f), _np.ones((1, L), f)]),
        "w2a": _np.concatenate([g["attn_w2"].T, g["attn_b2"][None]]),
        "ident": _np.eye(P, dtype=f), "w_in_t": g["attn_w_in"].T, "cols": cols,
        "rows": _np.concatenate([g["attn_filt_decay"].ravel(), g["attn_filt_bias"].ravel(), g["attn_b_out"],
                                 g["ffn_e_score_correction_bias"]]),
        "consts": consts.astype(f), "fwd_hi": half(fwd).astype(f), "fwd_lo": half(fwd - half(fwd)).astype(f),
        "inv_hi": half(inv).astype(f), "inv_lo": half(inv - half(inv)).astype(f), "w_out_t": g["attn_w_out"].T,
        "gate_w_t": g["ffn_gate_weight"].T,
        "w_experts": _np.concatenate([_np.concatenate([gu, dn], 2), shared[:, None]], 1),
    }
    nc = _bacc.Bacc("TRN2", target_bir_lowering=False, num_devices=1)
    args, feed = {}, {}
    for name, a in arrays.items():
        feed[f"in_{name}"] = _np.ascontiguousarray(a)
        args[name] = nc.dram_tensor(f"in_{name}", a.shape, _mybir.dt.from_np(a.dtype), kind="ExternalInput").ap()
    out = nc.dram_tensor("out_0", (B, L, D), _mybir.dt.float32, kind="ExternalOutput").ap()
    build(nc, args, out)
    r = _run(nc, [feed], core_ids=[0])
    return r.results[0]["out_0"]
```

```python
from contextlib import ExitStack

import concourse.bass as bass
import numpy as np
from concourse import mybir

F32 = mybir.dt.float32
F32R = mybir.dt.float32r
U32 = mybir.dt.uint32
I32 = mybir.dt.int32
ALU = mybir.AluOpType
ACT = mybir.ActivationFunctionType
AX_X = mybir.AxisListType.X

P = 128
B, L, D = 4, 512, 128
NJ = L // P
NT = B * NJ
NK = NJ // 2
LH = L // 2
HB = B // 2
HW = HB * D
STEPS = 4
SLOTS = 3
ORDER = 2
GROUPS = ORDER + 1
EMB, HID = 33, 64
E, TOP_K, N_GROUP, TOPK_GROUP = 32, 6, 8, 4
GS = E // N_GROUP
ROUTED_SCALE = 2.5
INTER = 64
PAIRS = E // 2
NU = PAIRS + 1
EPS = 1e-5
MAX8 = 8
BIG = 3.0e38
FREQ = 10.0
ROUND = 1.5 * 2.0 ** 23
ROOT_BITS = float(0x5F3759DF)
TWO_PI = (6.28125, 1.9340515136718750e-03, 1.2556659146298881e-06)
PI = 3.1415925
USLOTS = 3
HSLOTS = 5
WSLOTS = 4
LAG = 3
SCALE_AT = ((0, 1), (0, 2), (0, 3))
NORMED_AT = ((0, 4), (0, 5), (0, 6), (0, 7))
TURNED_AT = ((0, 6), (0, 9))
SCALED_AT = ((0, 6), (0, 9))
LOGITS_AT = ((0, 8), (0, 11))
LOGITS_COPIED_AT = ((0, 8), (0, 11))
ROUTE_AT = ((0, 6), (1, 1), (1, 8))
WEIGHTS_TURNED_AT = ((0, 13), (1, 7), (1, 14))
WEIGHTS_COPIED_AT = ((0, 13), (1, 7), (1, 14))
LATE_CHUNK_AT = (0, 2)
EARLY_CHUNKS = 2
CHUNK = 2


def build(nc, io, out):
    ctx = ExitStack()
    with ctx:
        def sem(name):
            return ctx.enter_context(nc.semaphore(name))

        def sb(name, shape, dt=F32):
            return ctx.enter_context(nc.sbuf_tensor(name, shape, dt))

        def overlay(region, *groups):
            got, most = {}, 0
            for group in groups:
                with ExitStack() as inner:
                    words = 0
                    for name, shape, dt in group:
                        got[name] = inner.enter_context(nc.sbuf_tensor(name, shape, dt))
                        words += int(np.prod(shape[1:]))
                    most = max(most, words)
            sb(region, [P, most + 16])
            return got

        GATE_BANKS, UP_BANKS = (0, 1, 4), (2, 3, 5)
        FILTER_ODD, FILTER_EVEN = (7, 3), (6, 2)
        STEP_ODD, STEP_EVEN = (4, 2), (5, 3)
        bank = [ctx.enter_context(nc.psum_tensor(f"bank{i}", [P, 512], F32)) for i in range(8)]

        x = sb("x", [P, B, NJ, D])
        fwd_hi = sb("fwd_hi", [P, 2, NK, 2, LH], F32R)
        fwd_lo = sb("fwd_lo", [P, 2, NK, 2, LH], F32R)
        inv_hi = sb("inv_hi", [P, 2, NK, 2, LH], F32R)
        inv_lo = sb("inv_lo", [P, 2, NK, 2, LH], F32R)
        SETUP_WORDS = 2 * NJ * ORDER * D + B * L
        weights = overlay(
            "region_weights",
            [("w_hi", [P, NU, 3, D], F32R), ("w_lo", [P, NU, 3, D], F32R)],
            [("not_used", [P, 2 * NU * 3 * D - SETUP_WORDS], F32), ("h_hi", [P, NJ, ORDER * D], F32R),
             ("h_lo", [P, NJ, ORDER * D], F32R), ("h_t", [P, B, L], F32)],
        )
        w_hi, w_lo, h_hi, h_lo, h_t = (weights[k] for k in ("w_hi", "w_lo", "h_hi", "h_lo", "h_t"))
        v = sb("v", [P, B, L])
        tok_hi = sb("tok_hi", [P, NJ, B, D], F32R)
        tok_lo = sb("tok_lo", [P, NJ, B, D], F32R)
        w_stage = sb("w_stage", [P, 2, CHUNK, 3, D])
        ident = sb("ident", [P, P])
        w_in_t = sb("w_in_t", [P, GROUPS * D])
        w_out_t = sb("w_out_t", [P, D])
        w_out_g = sb("w_out_g", [P, B, D])
        gate_w_t = sb("gate_w_t", [P, E])
        cols = sb("cols", [P, 15])
        tap_bias = sb("tap_bias", [P, 3, GROUPS])
        conv_bias = sb("conv_bias", [P, 3, GROUPS])
        consts = sb("consts", [P, 16])
        rows = sb("rows", [P, 672])
        modT = sb("modT", [P, 6, B])
        stats = sb("stats", [P, NT, 6])
        mv = sb("mv", [P, NT, 2])
        var_eps = sb("var_eps", [P, NT])
        bias_col = sb("bias_col", [P, NT])
        rstd = sb("rstd", [P, NT])
        newton = sb("newton", [P, NT])
        c_t = sb("c_t", [P, B])
        silu_c = sb("silu_c", [P, B])
        sign = sb("sign", [P, B])

        big = overlay(
            "region_spectra",
            [("decay", [P, NJ, ORDER * D], F32),
             ("wmod", [P, 6 * D], F32)],
            [("y_hi", [P, SLOTS, 2, 2 * HW], F32R), ("y_lo", [P, SLOTS, 2, 2 * HW], F32R), ("gap", [P, 16], F32),
             ("odd", [P, 2 * HW], F32), ("folded", [P, 2, 2 * HW], F32)],
            [("silu_g", [P, USLOTS, L], F32), ("act", [P, USLOTS, L], F32),
             ("act_hi", [P, HSLOTS, L], F32R), ("act_lo", [P, HSLOTS, L], F32R), ("moe_t", [P, L], F32)],
        )
        mid = overlay(
            "region_gates",
            [("gates", [P, ORDER, B, L], F32)],
            [("xhat", [P, NT, D], F32), ("comb_t", [E, NT * P], F32)],
        )
        gates, xhat, comb_t = (mid[k] for k in ("gates", "xhat", "comb_t"))
        small = overlay(
            "region_products",
            [("silu_rep", [P, B, P], F32), ("ga", [P, B, D], F32),
             ("ga_sign", [P, B, D], F32), ("turns", [HID, L], F32), ("angle", [HID, L], F32)],
            [("y", [P, NK, 2, 2 * HW], F32), ("cross", [P, 2, 2 * HW], F32), ("even_odd", [P, 2, 2 * HW], F32)],
            [("scores", [P, NT, E], F32), ("biased", [P, NT, E], F32), ("group_max", [P, NT, N_GROUP + TOPK_GROUP], F32),
             ("group_left", [P, NT, N_GROUP + TOPK_GROUP], F32), ("group_in", [P, NT, N_GROUP], F32),
             ("masked", [P, NT, E + 2], F32), ("left", [P, NT, E + 2], F32), ("top8", [P, NT, MAX8], F32),
             ("weight_sum", [P, NT], F32), ("comb", [P, NT, E], F32)],
        )
        filt = overlay(
            "region_filter",
            [("pos_t", [EMB + 1, L], F32), ("w1a", [EMB + 1, HID], F32), ("w2a", [HID + 1, ORDER * D], F32),
             ("wave", [HID + 1, L], F32)],
            [("filt_c", [P, ORDER, NJ, D], F32), ("filt_s", [P, ORDER, NJ, D], F32)],
            [("pair_weights", [P, WSLOTS, L], F32)],
        )
        filt_c, filt_s, pair_weights = filt["filt_c"], filt["filt_s"], filt["pair_weights"]
        decay, wmod, y_hi, y_lo, odd, folded = (
            big[k] for k in ("decay", "wmod", "y_hi", "y_lo", "odd", "folded"))
        silu_g, act, act_hi, act_lo = (big[k] for k in ("silu_g", "act", "act_hi", "act_lo"))
        moe_t = big["moe_t"]
        silu_rep, ga, ga_sign, turns, angle = (
            small[k] for k in ("silu_rep", "ga", "ga_sign", "turns", "angle"))
        y, cross, even_odd = small["y"], small["cross"], small["even_odd"]
        scores, biased, group_max, group_left, group_in = (
            small[k] for k in ("scores", "biased", "group_max", "group_left", "group_in"))
        masked, left, top8, weight_sum, comb = (small[k] for k in ("masked", "left", "top8", "weight_sum", "comb"))
        pos_t, w1a, w2a, wave = (filt[k] for k in ("pos_t", "w1a", "w2a", "wave"))

        h_time = decay
        x_tiles = x[:].rearrange("p b j d -> p (b j) d")
        h2 = v
        h2_hi = tok_hi[:].rearrange("p j b d -> p (j b d)").rearrange("p (b l) -> p b l", b=B)
        h2_lo = tok_lo[:].rearrange("p j b d -> p (j b d)").rearrange("p (b l) -> p b l", b=B)
        SA, CA, GA, SB, CB, GB = range(6)
        DECAY, FBIAS, BOUT, CORR = slice(0, 256), slice(256, 512), slice(512, 640), slice(640, 672)

        mod_in, filt_in, const_in, proj_in, late_in = (
            sem(n) for n in ("mod_in", "filt_in", "const_in", "proj_in", "late_in"))
        pair_in = [sem(f"pair_in{i}") for i in range(WSLOTS)]
        x_in = [sem(f"x_in{b}") for b in range(B)]
        c_in, dft_in, inv_in, conv_bias_done = sem("c_in"), sem("dft_in"), sem("inv_in"), sem("conv_bias_done")
        n_chunks = -(-NU // CHUNK)
        w_in_sem = [sem(f"w_in{i}") for i in range(2)]
        silu_c_done, rep_done, mod_mm, ga_mm, ga_copied, mod_done, ga_done, zero_done = (
            sem(n) for n in ("silu_c_done", "rep_done", "mod_mm", "ga_mm", "ga_copied", "mod_done", "ga_done", "zero_done"))
        rstd_done, xhat_done, xhat_t, h_t_done = (
            sem(n) for n in ("rstd_done", "xhat_done", "xhat_t", "h_t_done"))
        proj_mm, mid_done, gates_done, v_done = (
            sem(n) for n in ("proj_mm", "mid_done", "gates_done", "v_done"))
        z_mm, angle_in, angle_done, wave_done, decay_done, h_mm, h_done, h_hi_done, h_lo_done, filt_done = (
            sem(n) for n in ("z_mm", "angle_in", "angle_done", "wave_done", "decay_done", "h_mm", "h_done",
                             "h_hi_done", "h_lo_done", "filt_done"))
        w_hi_done, w_lo_done = sem("w_hi_done"), sem("w_lo_done")
        v_t, tok_hi_done, tok_lo_done, odd_mm, even_mm, odd_copied, folded_done, prod_done = (
            sem(n) for n in ("v_t", "tok_hi_done", "tok_lo_done", "odd_mm", "even_mm", "odd_copied", "folded_done",
                             "prod_done"))
        y_done, even_odd_done, y_hi_done, y_lo_done, inv_mm = (
            sem(n) for n in ("y_done", "even_odd_done", "y_hi_done", "y_lo_done", "inv_mm"))
        logits_copied, tables_done = sem("logits_copied"), sem("tables_done")
        attn_mm, x1_done, h2_done, h2_hi_done, h2_lo_done, logits_mm, scores_done, comb_done, comb_tr, comb_t_done = (
            sem(n) for n in ("attn_mm", "x1_done", "h2_done", "h2_hi_done", "h2_lo_done", "logits_mm", "scores_done",
                             "comb_done", "comb_tr", "comb_t_done"))
        gate_mm, up_mm, down_mm, silu_done, gated_done, act_done, act_hi_done, act_lo_done = (
            sem(n) for n in ("gate_mm", "up_mm", "down_mm", "silu_done", "gated_done", "act_done",
                             "act_hi_done", "act_lo_done"))
        moe_done, moe_tr, out_done, stored = (sem(n) for n in ("moe_done", "moe_tr", "out_done", "stored"))
        dve_chain, act_chain, pool_chain = sem("dve_chain"), sem("act_chain"), sem("pool_chain")

        block = ctx.enter_context(nc.Block())

        def chunk_units(q):
            return q * CHUNK, min(NU, (q + 1) * CHUNK)

        def unit(b, u):
            return NU * b + u + 1

        def before(u):
            return u - USLOTS if u >= USLOTS else max(r for r in range(NU) if r % USLOTS == u % USLOTS) - NU

        def half_slot(u):
            return HSLOTS - 1 if u == PAIRS else u % (HSLOTS - 1)

        def half_before(u):
            return max(r for r in range(-NU, u) if half_slot(r % NU) == half_slot(u))

        def conv_place(m):
            return (GROUPS - 1, m) if m < B else ((m - B) // B, m % B)

        def conv_out(m):
            return v[:, m] if m < B else gates[:, (m - B) // B, m % B]

        def conv_bank(m):
            return bank[2 + m if m < B else m % 2 if m in step_projections(1) else 6 + m % 2]

        def step_projections(s):
            return (B + 2 * s, B + 2 * s + 1)

        def step_batches(s):
            return range(HB * (s % 2), HB * (s % 2) + HB)

        def slot(s, kt):
            return (NK * s + kt) % SLOTS

        def slot_reader(s, kt):
            q = NK * s + kt - SLOTS
            return q // NK if q >= 0 else None

        @block.sync
        def _(sp):
            def load_x(b):
                sp.dma_start(x[:, b], io["x"][b].rearrange("(j p) d -> p j d", p=P)).then_inc(x_in[b], 16)

            sp.dma_start(c_t[:], io["c_t"]).then_inc(c_in, 16)
            load_x(0)
            sp.dma_start(wmod[:], io["wmod"]).then_inc(mod_in, 16)
            load_x(1)
            sp.dma_start(w1a[:], io["w1a"]).then_inc(filt_in, 16)
            sp.dma_start(pos_t[:], io["pos_t"]).then_inc(filt_in, 16)
            load_x(2)
            load_x(3)
            sp.dma_start(cols[:], io["cols"]).then_inc(proj_in, 16)
            sp.dma_start(ident[:], io["ident"]).then_inc(proj_in, 16)
            sp.dma_start(w_in_t[:], io["w_in_t"]).then_inc(proj_in, 16)
            sp.dma_start(w_out_t[:], io["w_out_t"]).then_inc(proj_in, 16)
            sp.dma_start(w2a[:], io["w2a"]).then_inc(filt_in, 16)
            sp.dma_start(rows[:], io["rows"].rearrange("(a n) -> a n", a=1).to_broadcast([P, 672])).then_inc(const_in, 16)
            sp.dma_start(consts[:], io["consts"]).then_inc(const_in, 16)
            sp.dma_start(gate_w_t[:], io["gate_w_t"]).then_inc(late_in, 16)

            def load_weights(q):
                a, z = chunk_units(q)
                if q >= 2:
                    sp.wait_ge(w_lo_done, q - 1)
                sp.dma_start(w_stage[:, q % 2, 0:z - a], io["w_experts"][:, a:z]).then_inc(w_in_sem[q % 2], 16)

            for q in range(n_chunks - 1):
                load_weights(q)
            sp.wait_ge(prod_done, NK * STEPS)

            def store(b):
                sp.wait_ge(out_done, b)
                sp.dma_start(out[bass.ds(b - 1, 1)].rearrange("o (j p) d -> p (o j) d", p=P),
                             x[:, bass.ds(b - 1, 1)].rearrange("p o j d -> p (o j) d")).then_inc(stored, 16)

            def spread_weights(b, first):
                for u in range(PAIRS):
                    if not first or u >= WSLOTS:
                        sp.wait_ge(act_done, unit(b, u - WSLOTS if u >= WSLOTS else u - WSLOTS + PAIRS - NU))
                    for i in range(2):
                        e = 2 * u + i
                        sp.dma_start(pair_weights[i * INTER:(i + 1) * INTER, u % WSLOTS],
                                     comb_t[e:e + 1, bass.ds(b * L, L)].unsqueeze(1).to_broadcast([1, INTER, L])
                                     ).then_inc(pair_in[u % WSLOTS], 16)
                    if u == WSLOTS - 1 and first:
                        load_weights(n_chunks - 1)
                    if u == PAIRS // 2 and not first:
                        store(b)

            sp.wait_ge(comb_t_done, 1)
            spread_weights(0, True)
            sp.wait_ge(comb_t_done, 2)
            spread_weights(1, False)
            sp.wait_ge(comb_t_done, B)
            with sp.Fori(2, B) as b:
                spread_weights(b, False)
            store(B)
            sp.wait_ge(stored, 16 * B)

        @block.gpsimd
        def _(pool):
            gp = nc.gpsimd
            chain = [0]

            def link(ins):
                chain[0] += 1
                ins.then_inc(pool_chain, 1)
                pool.wait_ge(pool_chain, chain[0])

            gp.memset(wave[HID:HID + 1], 1.0).then_inc(zero_done, 1)
            pool.wait_ge(zero_done, 1)
            pool.wait_ge(x_in[B - 1], 16)
            pool.dma_start(fwd_hi[:], io["fwd_hi"].bitcast(F32R)).then_inc(dft_in, 16)
            pool.dma_start(fwd_lo[:], io["fwd_lo"].bitcast(F32R)).then_inc(dft_in, 16)
            pool.dma_start(inv_hi[:], io["inv_hi"].bitcast(F32R)).then_inc(inv_in, 16)
            pool.dma_start(inv_lo[:], io["inv_lo"].bitcast(F32R)).then_inc(inv_in, 16)
            pool.wait_ge(ga_copied, 1)
            link(gp.tensor_scalar(ga_sign[:], ga[:], 0.0, 2.0, ALU.is_ge, ALU.mult))
            link(gp.tensor_scalar(ga_sign[:], ga_sign[:], -1.0, None, ALU.add))
            link(gp.tensor_tensor(ga[:], ga[:], ga_sign[:], ALU.mult))
            link(gp.tensor_scalar(ga[:], ga[:], 0.25, None, ALU.max))
            link(gp.tensor_tensor(ga[:], ga[:], ga_sign[:], ALU.mult))
            pool.wait_ge(proj_in, 64)
            link(gp.tensor_tensor(w_out_g[:], ga[:], w_out_t[:].unsqueeze(1).to_broadcast([P, B, D]), ALU.mult))
            pool.wait_ge(const_in, 32)
            link(gp.tensor_tensor(ga[:], ga[:], rows[:, BOUT].unsqueeze(1).to_broadcast([P, B, D]), ALU.mult))
            for b in range(B):
                pool.wait_ge(xhat_done, b + 1)
                gp.tensor_tensor(x[:, b], x[:, b], ga[:, b].unsqueeze(1).to_broadcast([P, NJ, D]),
                                 ALU.add).then_inc(ga_done, 1)

            def split_weights(q):
                a, z = chunk_units(q)
                pool.wait_ge(w_hi_done, q + 1)
                if z * 3 * D > NU * 3 * D - SETUP_WORDS:
                    pool.wait_ge(proj_mm, GROUPS * B)
                gp.tensor_tensor(w_lo[:, a:z], w_stage[:, q % 2, 0:z - a], w_hi[:, a:z].bitcast(F32),
                                 ALU.subtract).then_inc(w_lo_done, 1)

            def split_h2(b):
                pool.wait_ge(h2_hi_done, b + 1)
                gp.tensor_tensor(h2_lo[:, b], h2[:, b], h2_hi[:, b].bitcast(F32),
                                 ALU.subtract).then_inc(h2_lo_done, 1)

            for q in range(EARLY_CHUNKS):
                split_weights(q)
            for s in range(STEPS):
                for kt in range(NK):
                    q = NK * s + kt
                    pool.wait_ge(y_done, q + 1)
                    if q:
                        pool.wait_ge(y_lo_done, 2 * q)
                    gp.tensor_tensor(even_odd[:, 0], y[:, kt, 0], y[:, kt, 1], ALU.add).then_inc(even_odd_done, 1)
                    gp.tensor_tensor(even_odd[:, 1], y[:, kt, 0], y[:, kt, 1], ALU.subtract).then_inc(even_odd_done, 1)
                    for par in range(2):
                        pool.wait_ge(even_odd_done, 2 * q + par + 1)
                        pool.wait_ge(y_hi_done, 2 * q + par + 1)
                        gp.tensor_tensor(y_lo[:, slot(s, kt), par], even_odd[:, par],
                                         y_hi[:, slot(s, kt), par].bitcast(F32), ALU.subtract).then_inc(y_lo_done, 1)
                if 1 <= s < STEPS - 1:
                    split_weights(EARLY_CHUNKS + s - 1)
            pool.wait_ge(y_lo_done, 2 * NK * STEPS)
            link(gp.memset(group_max[:], BIG))
            link(gp.memset(masked[:, :, 0:E], 0.0))
            gp.memset(masked[:, :, E:E + 2], BIG).then_inc(tables_done, 1)
            for q in range(EARLY_CHUNKS + 2, n_chunks - 3):
                split_weights(q)
            for b in range(HB):
                split_h2(b)
                split_weights(n_chunks - 3 + b)

            def experts(b):
                for u in range(NU):
                    pool.wait_ge(act_hi_done, unit(b, u))
                    gp.tensor_tensor(act_lo[:, half_slot(u)], act[:, u % USLOTS], act_hi[:, half_slot(u)].bitcast(F32),
                                            ALU.subtract).then_inc(act_lo_done, 1)
                    if isinstance(b, int) and (b, u) == LATE_CHUNK_AT:
                        split_weights(n_chunks - 1)
                    if isinstance(b, int) and (b, u) in SCALED_AT:
                        split_h2(HB + SCALED_AT.index((b, u)))

            experts(0)
            with pool.Fori(1, B) as b:
                experts(b)

        @block.scalar
        def _(act_e):
            sc = nc.scalar
            act_e.wait_ge(c_in, 16)
            sc.activation(silu_c[:], c_t[:], ACT.Silu).then_inc(silu_c_done, 1)
            act_e.wait_ge(z_mm, 1)
            sc.activation(angle[:], bank[6][0:HID, :], ACT.Copy, scale=FREQ).then_inc(angle_in, 1)
            act_e.wait_ge(ga_mm, 1)
            sc.activation(ga[:].rearrange("p b d -> p (b d)"), bank[7][:], ACT.Copy).then_inc(ga_copied, 1)
            act_e.wait_ge(const_in, 32)
            sc.activation(rows[:, DECAY], rows[:, DECAY], ACT.Exp).then_inc(act_chain, 1)
            act_e.wait_ge(act_chain, 1)
            for j in range(NJ):
                sc.activation(decay[:, j], rows[:, DECAY], ACT.Exp, scale=consts[:, j:j + 1]).then_inc(decay_done, 1)
            act_e.wait_ge(mod_done, 1)
            for b in range(B):
                act_e.wait_ge(xhat_t, b + 1)
                sc.activation(h_t[:, b], bank[b % 2][:], ACT.Identity, bias=modT[:, SA, b:b + 1],
                              scale=modT[:, CA, b:b + 1]).then_inc(h_t_done, 1)
            act_e.wait_ge(angle_done, 1)
            sc.activation(wave[0:HID], angle[:], ACT.Sin).then_inc(wave_done, 1)
            act_e.wait_ge(conv_bias_done, 1)

            def project(m):
                g, _ = conv_place(m)
                act_e.wait_ge(proj_mm, m + 1)
                for i, cut in enumerate((slice(0, 1), slice(1, L - 1), slice(L - 1, L))):
                    last = sc.activation(conv_out(m)[:, cut], conv_bank(m)[:, cut], ACT.Identity,
                                         bias=conv_bias[:, i, g:g + 1], scale=cols[:, 6 + g:7 + g])
                last.then_inc(mid_done, 1)

            for m in range(B - 1):
                project(m)
            act_e.wait_ge(h_done, 1)
            sc.activation(h_hi[:], h_time[:], ACT.Copy).then_inc(h_hi_done, 1)
            project(B - 1)

            def split_weights(q):
                a, z = chunk_units(q)
                act_e.wait_ge(w_in_sem[q % 2], 16 * (q // 2 + 1))
                sc.activation(w_hi[:, a:z], w_stage[:, q % 2, 0:z - a], ACT.Copy).then_inc(w_hi_done, 1)

            def copy_odd(q, bank_odd):
                act_e.wait_ge(odd_mm, q + 1)
                if q:
                    act_e.wait_ge(folded_done, 2 * q)
                sc.activation(odd[:], bank_odd[:], ACT.Copy).then_inc(odd_copied, 1)

            def split_tokens(s, b):
                act_e.wait_ge(v_t, HB * s + b % HB + 1)
                sc.activation(tok_hi[:, :, b], bank[b % 2][:].rearrange("p (j d) -> p j d", j=NJ),
                              ACT.Copy).then_inc(tok_hi_done, 1)

            copy_odd(0, bank[FILTER_ODD[0]])
            for b in range(HB):
                split_tokens(0, b)
            copy_odd(1, bank[FILTER_ODD[1]])
            for q in range(EARLY_CHUNKS):
                split_weights(q)

            def split_spectra(q):
                s, kt = divmod(q, NK)
                if slot_reader(s, kt) is not None:
                    act_e.wait_ge(inv_mm, HB * (slot_reader(s, kt) + 1))
                for par in range(2):
                    act_e.wait_ge(even_odd_done, 2 * q + par + 1)
                    sc.activation(y_hi[:, slot(s, kt), par], even_odd[:, par], ACT.Copy).then_inc(y_hi_done, 1)

            for s in range(STEPS):
                if s >= 2:
                    for b in step_batches(s):
                        split_tokens(s, b)
                    for m in step_projections(s):
                        project(m)
                if s == 1:
                    copy_odd(NK + NK * s, bank[STEP_ODD[0]])
                if s:
                    split_spectra(NK * s - 1)
                if s != 1:
                    copy_odd(NK + NK * s, bank[STEP_ODD[0]])
                if s == 0:
                    for b in step_batches(1):
                        split_tokens(1, b)
                copy_odd(NK + NK * s + 1, bank[STEP_ODD[1]])
                if s < 2:
                    for m in step_projections(s):
                        project(m)
                split_spectra(NK * s)
                if s < STEPS - 1:
                    split_weights(2 + s)
            split_spectra(NK * STEPS - 1)
            split_weights(n_chunks - 4)

            def normalise(b, tiles=range(NJ)):
                act_e.wait_ge(rstd_done, b + 1)
                for j in tiles:
                    t = b * NJ + j
                    last = sc.activation(xhat[:, t], x_tiles[:, t], ACT.Identity, bias=bias_col[:, t:t + 1],
                                         scale=rstd[:, t:t + 1])
                if tiles[-1] == NJ - 1:
                    last.then_inc(xhat_done, 1)

            def scale_by_channel(b):
                act_e.wait_ge(xhat_t, B + b + 1)
                sc.activation(h2[:, b], bank[b if b < HB else 7][:], ACT.Identity, bias=modT[:, SB, b:b + 1],
                              scale=modT[:, CB, b:b + 1]).then_inc(h2_done, 1)
                act_e.wait_ge(h2_done, b + 1)
                sc.activation(h2_hi[:, b], h2[:, b], ACT.Copy).then_inc(h2_hi_done, 1)

            def batch_scores(b):
                return scores[:, b * NJ:(b + 1) * NJ].rearrange("p t e -> p (t e)")

            def logits_out(b):
                act_e.wait_ge(logits_mm, b + 1)
                if b < HB:
                    sc.activation(batch_scores(b), bank[4][:, b * NJ * E:(b + 1) * NJ * E],
                                  ACT.Sigmoid).then_inc(scores_done, 1)
                else:
                    sc.activation(batch_scores(b), bank[7][:, 0:NJ * E], ACT.Copy).then_inc(logits_copied, 1)
                if b == B - 1:
                    act_e.wait_ge(logits_copied, B - HB)
                    late = scores[:, HB * NJ:NT].rearrange("p t e -> p (t e)")
                    sc.activation(late, late, ACT.Sigmoid).then_inc(scores_done, 2)

            def weights_by_expert(b):
                act_e.wait_ge(comb_tr, b + 1)
                sc.activation(comb_t[:, b * L:(b + 1) * L], bank[7 if b else 5][0:E, :],
                              ACT.Copy).then_inc(comb_t_done, 1)

            act_e.wait_ge(y_lo_done, 2 * NK * STEPS)
            normalise(0)
            scale_by_channel(0)
            logits_out(0)
            normalise(1)
            split_weights(n_chunks - 3)
            scale_by_channel(1)
            logits_out(1)
            split_weights(n_chunks - 2)
            weights_by_expert(0)

            def high(b, d):
                act_e.wait_ge(act_done, unit(b, d))
                u = d % NU
                last_user = half_before(u) + d - u
                if not isinstance(b, int) or NU * b + last_user >= 0:
                    act_e.wait_ge(down_mm, unit(b, last_user))
                sc.activation(act_hi[:, half_slot(u)], act[:, u % USLOTS], ACT.Copy).then_inc(act_hi_done, 1)

            def moe_sum(b):
                act_e.wait_ge(down_mm, unit(b, -1))
                sc.activation(moe_t[:], bank[6][:], ACT.Copy, scale=modT[:, GB, bass.ds(b - 1, 1)]).then_inc(moe_done, 1)

            def experts(b, first):
                for u in range(NU):
                    if u == LAG and not first:
                        moe_sum(b)
                    act_e.wait_ge(gate_mm, unit(b, u))
                    sc.activation(silu_g[:, u % USLOTS], bank[GATE_BANKS[u % USLOTS]][:], ACT.Silu).then_inc(silu_done, 1)
                    if u >= 1 or not first:
                        high(b, u - 1)
                    if isinstance(b, int):
                        if (b, u) == LATE_CHUNK_AT:
                            split_weights(n_chunks - 1)
                        if (b, u) in NORMED_AT:
                            late, half = divmod(NORMED_AT.index((b, u)), 2)
                            normalise(HB + late, range(half * NJ // 2, (half + 1) * NJ // 2))
                        if (b, u) in SCALED_AT:
                            scale_by_channel(HB + SCALED_AT.index((b, u)))
                        if (b, u) in LOGITS_COPIED_AT:
                            logits_out(HB + LOGITS_COPIED_AT.index((b, u)))
                        if (b, u) in WEIGHTS_COPIED_AT:
                            weights_by_expert(1 + WEIGHTS_COPIED_AT.index((b, u)))

            experts(0, True)
            experts(1, False)
            with act_e.Fori(2, B) as b:
                experts(b, False)
            high(B, -1)
            moe_sum(B)

        @block.vector
        def _(dve):
            ve = nc.vector
            chain = [0]

            def link(ins):
                chain[0] += 1
                ins.then_inc(dve_chain, 1)
                dve.wait_ge(dve_chain, chain[0])

            def tile_stats(b):
                for t in range(b * NJ, (b + 1) * NJ):
                    last = ve.bn_stats(stats[:, t], x_tiles[:, t])
                link(last)
                for t in range(b * NJ, (b + 1) * NJ):
                    last = ve.bn_aggr(mv[:, t], stats[:, t])
                link(last)

            def norm_guess(at):
                link(ve.tensor_scalar(var_eps[:, at], mv[:, at, 1], EPS, None, ALU.add))
                link(ve.tensor_scalar(rstd[:, at].bitcast(I32), var_eps[:, at].bitcast(I32), -0.5, ROOT_BITS,
                                      ALU.mult, ALU.add))

            def newton_step(at):
                link(ve.tensor_tensor(newton[:, at], rstd[:, at], rstd[:, at], ALU.mult))
                link(ve.scalar_tensor_tensor(newton[:, at], newton[:, at], -0.5, var_eps[:, at], ALU.mult, ALU.mult))
                link(ve.scalar_tensor_tensor(rstd[:, at], newton[:, at], 1.5, rstd[:, at], ALU.add, ALU.mult))

            def norm_scale(at):
                norm_guess(at)
                for _ in range(3):
                    newton_step(at)

            dve.wait_ge(silu_c_done, 1)
            ve.tensor_copy(silu_rep[:], silu_c[:].unsqueeze(2).to_broadcast([P, B, P])).then_inc(rep_done, 1)
            for b in range(2):
                dve.wait_ge(x_in[b], 16)
                tile_stats(b)
            dve.wait_ge(mod_mm, 1)
            link(ve.tensor_copy(modT[:].rearrange("p m b -> p (m b)"), bank[6][:, 0:6 * B]))
            ve.tensor_scalar(modT[:, CA], modT[:, CA], 1.0, None, ALU.add)
            ve.tensor_scalar(modT[:, CB], modT[:, CB], 1.0, None, ALU.add)
            link(ve.tensor_scalar(sign[:], modT[:, GB], 0.0, 2.0, ALU.is_ge, ALU.mult))
            link(ve.tensor_scalar(sign[:], sign[:], -1.0, None, ALU.add))
            link(ve.tensor_tensor(modT[:, GB], modT[:, GB], sign[:], ALU.mult))
            ve.scalar_tensor_tensor(modT[:, GB], modT[:, GB], 0.25, sign[:], ALU.max, ALU.mult).then_inc(mod_done, 1)
            for b in range(2, B):
                dve.wait_ge(x_in[b], 16)
                tile_stats(b)
            norm_scale(slice(0, NT))
            for b in range(B):
                for t in range(b * NJ, (b + 1) * NJ):
                    last = ve.tensor_scalar(xhat[:, t], x_tiles[:, t], mv[:, t, 0:1], rstd[:, t:t + 1],
                                            ALU.subtract, ALU.mult)
                last.then_inc(xhat_done, 1)
            dve.wait_ge(angle_in, 1)
            link(ve.tensor_scalar(turns[:], angle[:], float(1 / (2 * np.pi)), ROUND, ALU.mult, ALU.add))
            link(ve.tensor_scalar(turns[:], turns[:], -ROUND, None, ALU.add))
            for part in TWO_PI:
                link(ve.scalar_tensor_tensor(angle[:], turns[:], -part, angle[:], ALU.mult, ALU.add))
            ve.tensor_scalar(angle[:], angle[:], PI, -PI, ALU.min, ALU.max).then_inc(angle_done, 1)
            dve.wait_ge(proj_in, 64)
            taps = cols[:, 3:12].rearrange("p (k g) -> p k g", k=3)
            link(ve.tensor_tensor(tap_bias[:], taps, cols[:, 0:3].unsqueeze(1).to_broadcast([P, 3, GROUPS]), ALU.mult))
            link(ve.tensor_tensor(conv_bias[:, 1], tap_bias[:, 1], cols[:, 12:15], ALU.add))
            ve.tensor_tensor(conv_bias[:, 0], conv_bias[:, 1], tap_bias[:, 2], ALU.add)
            link(ve.tensor_tensor(conv_bias[:, 2], conv_bias[:, 1], tap_bias[:, 0], ALU.add))
            ve.tensor_tensor(conv_bias[:, 1], conv_bias[:, 2], tap_bias[:, 2], ALU.add).then_inc(conv_bias_done, 1)
            for j in range(NJ):
                dve.wait_ge(h_mm, j // 2 + 1)
                dve.wait_ge(decay_done, j + 1)
                link(ve.tensor_tensor(h_time[:, j], bank[6 + j // 2][:, (j % 2) * 256:(j % 2 + 1) * 256], decay[:, j],
                                      ALU.mult))
                last = ve.tensor_tensor(h_time[:, j], h_time[:, j], rows[:, FBIAS], ALU.add)
            last.then_inc(h_done, 1)
            dve.wait_ge(h_hi_done, 1)
            ve.tensor_tensor(h_lo[:], h_time[:], h_hi[:].bitcast(F32), ALU.subtract).then_inc(h_lo_done, 1)

            def outer_taps(m):
                g, _ = conv_place(m)
                dst, src = conv_out(m), conv_bank(m)
                dve.wait_ge(mid_done, m + 1)
                link(ve.scalar_tensor_tensor(dst[:, 1:L], src[:, 0:L - 1], cols[:, 3 + g:4 + g], dst[:, 1:L],
                                             ALU.mult, ALU.add))
                ve.scalar_tensor_tensor(dst[:, 0:L - 1], src[:, 1:L], cols[:, 9 + g:10 + g], dst[:, 0:L - 1],
                                        ALU.mult, ALU.add).then_inc(v_done if m < B else gates_done, 1)

            def fold(q, bank_even):
                dve.wait_ge(even_mm, q + 1)
                dve.wait_ge(odd_copied, q + 1)
                ve.tensor_tensor(folded[:, 0], bank_even[:], odd[:], ALU.add).then_inc(folded_done, 1)
                ve.tensor_tensor(folded[:, 1], bank_even[:], odd[:], ALU.subtract).then_inc(folded_done, 1)
                dve.wait_ge(folded_done, 2 * q + 2)

            def rotate(kt):
                two = lambda a: a.rearrange("p (n d) -> p n d", n=ORDER)
                for side in range(2):
                    hc, hs = (two(folded[:, side, i * HW:(i + 1) * HW]) for i in ((0, 1), (1, 0))[side])
                    i = 2 * kt + side
                    cos, sin, neg = (consts[:, 4 * a + i:4 * a + i + 1] for a in (1, 2, 3))
                    ve.tensor_scalar(filt_c[:, :, i], hc, cos, None, ALU.mult)
                    link(ve.tensor_scalar(filt_s[:, :, i], hs, cos, None, ALU.mult))
                    ve.scalar_tensor_tensor(filt_c[:, :, i], hs, sin, filt_c[:, :, i], ALU.mult, ALU.add)
                    ve.scalar_tensor_tensor(filt_s[:, :, i], hc, neg, filt_s[:, :, i], ALU.mult,
                                            ALU.add).then_inc(filt_done, 1)

            def split_tokens(s, b):
                dve.wait_ge(tok_hi_done, HB * s + b % HB + 1)
                ve.tensor_tensor(tok_lo[:, :, b], bank[b % 2][:].rearrange("p (j d) -> p j d", j=NJ),
                                 tok_hi[:, :, b].bitcast(F32), ALU.subtract).then_inc(tok_lo_done, 1)

            def multiply_spectra(s, kt):
                n, q = s // 2, NK * s + kt
                shape = [P, 2, 2 * HB, D]
                tiles = lambda a: a.rearrange("p i (r d) -> p i r d", d=D)
                f = lambda a: a[:, n, 2 * kt:2 * kt + 2].unsqueeze(2).to_broadcast(shape)
                if s:
                    dve.wait_ge(even_odd_done, 2 * (q - NK) + 2)
                ve.tensor_tensor(tiles(y[:, kt]), tiles(folded[:]), f(filt_c), ALU.mult)
                ve.tensor_tensor(tiles(cross[:]), tiles(folded[:]), f(filt_s), ALU.mult).then_inc(prod_done, 1)

            def add_products(s, kt):
                dve.wait_ge(prod_done, NK * s + kt + 1)
                quarter = lambda a: a.rearrange("p side (i c) -> p (side i) c", i=2)
                dst, src = quarter(y[:, kt]), quarter(cross[:])
                ve.tensor_tensor(dst[:, 0:4:3], dst[:, 0:4:3], src[:, 1:3], ALU.subtract)
                ve.tensor_tensor(dst[:, 1:3], dst[:, 1:3], src[:, 0:4:3], ALU.add).then_inc(y_done, 1)

            def gate(s, b):
                by_parity = lambda a: a.rearrange("p (m par) -> p par m", par=2)
                dve.wait_ge(inv_mm, HB * s + b % HB + 1)
                ve.tensor_tensor(by_parity(v[:, b]), bank[6 + b % 2][:].rearrange("p (par m) -> p par m", par=2),
                                 by_parity(gates[:, s // 2, b]), ALU.mult).then_inc(v_done, 1)

            def residual(b):
                dve.wait_ge(attn_mm, b + 1)
                dve.wait_ge(ga_done, b + 1)
                ve.tensor_tensor(x[:, b].rearrange("p j d -> p (j d)"), bank[2 + b % 2][:],
                                 x[:, b].rearrange("p j d -> p (j d)"), ALU.add).then_inc(x1_done, 1)

            def second_shift(b, count):
                at = slice(b * NJ, (b + count) * NJ)
                ve.scalar_tensor_tensor(bias_col[:, at], mv[:, at, 0], -1.0, rstd[:, at],
                                        ALU.mult, ALU.mult).then_inc(rstd_done, count)

            def route_groups(b):
                at = slice(b * NJ, (b + 1) * NJ)
                dve.wait_ge(scores_done, b + 1)
                link(ve.tensor_tensor(biased[:, at], scores[:, at], rows[:, CORR].unsqueeze(1).to_broadcast([P, NJ, E]),
                                      ALU.add))
                link(ve.tensor_reduce(group_max[:, at, 0:N_GROUP], biased[:, at].rearrange("p t (g s) -> p t g s", g=N_GROUP),
                                      AX_X, ALU.max))
                for t in range(b * NJ, (b + 1) * NJ):
                    last = ve.max(top8[:, t], group_max[:, t])
                link(last)
                for t in range(b * NJ, (b + 1) * NJ):
                    last = ve.match_replace(group_left[:, t], top8[:, t], group_max[:, t], -BIG)
                link(last)
                link(ve.tensor_scalar(group_in[:, at], group_left[:, at, 0:N_GROUP], -BIG, None, ALU.is_equal))

            def route_experts(b):
                at = slice(b * NJ, (b + 1) * NJ)
                for s in range(GS):
                    last = ve.copy_predicated(masked[:, at, s:E:GS], group_in[:, at].bitcast(U32), biased[:, at, s:E:GS])
                link(last)
                for t in range(b * NJ, (b + 1) * NJ):
                    last = ve.max(top8[:, t], masked[:, t])
                link(last)
                for t in range(b * NJ, (b + 1) * NJ):
                    last = ve.match_replace(left[:, t], top8[:, t], masked[:, t], -BIG)
                link(last)

            def route_weights(b):
                at = slice(b * NJ, (b + 1) * NJ)
                link(ve.scalar_tensor_tensor(scores[:, at], left[:, at, 0:E], -BIG, scores[:, at], ALU.is_equal, ALU.mult))
                link(ve.tensor_reduce(weight_sum[:, at], scores[:, at], AX_X, ALU.add))
                link(ve.tensor_scalar(weight_sum[:, at], weight_sum[:, at], 1e-20, None, ALU.add))
                link(ve.reciprocal(weight_sum[:, at], weight_sum[:, at]))
                ve.scalar_tensor_tensor(comb[:, at], scores[:, at], ROUTED_SCALE,
                                        weight_sum[:, at].unsqueeze(2).to_broadcast([P, NJ, E]), ALU.mult,
                                        ALU.mult).then_inc(comb_done, 1)

            for m in range(B):
                outer_taps(m)
            for b in range(HB):
                split_tokens(0, b)
            for kt in range(NK):
                if kt:
                    dve.wait_ge(filt_done, 2 * kt)
                fold(kt, bank[FILTER_EVEN[kt]])
                rotate(kt)
            dve.wait_ge(filt_done, 2 * NK)
            dve.wait_ge(ga_done, B)
            for s in range(STEPS):
                for kt in range(NK):
                    if NK * s + kt:
                        dve.wait_ge(y_done, NK * s + kt)
                    fold(NK + NK * s + kt, bank[STEP_EVEN[kt]])
                    if s and kt == NK - 1:
                        for b in step_batches(s - 1):
                            gate(s - 1, b)
                    multiply_spectra(s, kt)
                    if s + kt == 0 or (1 <= s < STEPS - 1 and kt == NK - 1):
                        for b in step_batches(s + 1):
                            split_tokens(s + 1, b)
                    add_products(s, kt)
                    if (s, kt) in ((0, 1), (1, 0)):
                        for m in step_projections(s):
                            outer_taps(m)
                if 1 <= s < STEPS - 1:
                    for m in step_projections(s + 1):
                        outer_taps(m)
            for b in range(HB):
                residual(b)
                dve.wait_ge(x1_done, b + 1)
                tile_stats(b)
                norm_scale(slice(b * NJ, (b + 1) * NJ))
                second_shift(b, 1)
            gate(STEPS - 1, HB)
            dve.wait_ge(tables_done, 1)
            route_groups(0)
            route_experts(0)
            route_weights(0)
            gate(STEPS - 1, B - 1)
            for b in range(HB, B):
                residual(b)
            dve.wait_ge(x1_done, HB + 1)
            tile_stats(HB)

            def output(b):
                dve.wait_ge(moe_tr, b)
                done = x[:, bass.ds(b - 1, 1)].rearrange("p o j d -> p (o j d)")
                ve.tensor_tensor(done, bank[7][:], done, ALU.add).then_inc(out_done, 1)

            def experts(b, first):
                for u in range(NU):
                    dve.wait_ge(silu_done, unit(b, u))
                    dve.wait_ge(up_mm, unit(b, u))
                    if not first or u >= USLOTS:
                        dve.wait_ge(act_lo_done, unit(b, before(u)))
                    if u < PAIRS:
                        ve.tensor_tensor(act[:, u % USLOTS], bank[UP_BANKS[u % USLOTS]][:], silu_g[:, u % USLOTS],
                                         ALU.mult).then_inc(gated_done, 1)
                        dve.wait_ge(pair_in[u % WSLOTS], 32 * (PAIRS // WSLOTS * b + u // WSLOTS + 1))
                        dve.wait_ge(gated_done, PAIRS * b + u + 1)
                        ve.tensor_tensor(act[:, u % USLOTS], pair_weights[:, u % WSLOTS], act[:, u % USLOTS],
                                         ALU.mult).then_inc(act_done, 1)
                    else:
                        ve.tensor_tensor(act[:, u % USLOTS], bank[UP_BANKS[u % USLOTS]][:], silu_g[:, u % USLOTS],
                                         ALU.mult).then_inc(act_done, 1)
                    if u == LAG + 2 and not first:
                        output(b)
                    if isinstance(b, int):
                        if (b, u) == (0, 0):
                            dve.wait_ge(x1_done, B)
                            tile_stats(B - 1)
                        if (b, u) in SCALE_AT:
                            late = slice(HB * NJ, NT)
                            if (b, u) == SCALE_AT[0]:
                                norm_guess(late)
                            newton_step(late)
                            if (b, u) == SCALE_AT[-1]:
                                second_shift(HB, B - HB)
                        for r, (rb, ru) in enumerate(ROUTE_AT):
                            for step, route in enumerate((route_groups, route_experts, route_weights)):
                                if (b, u) == (rb, ru + step):
                                    route(1 + r)

            experts(0, True)
            experts(1, False)
            with dve.Fori(2, B) as b:
                experts(b, False)
            output(B)

        @block.tensor
        def _(pe):
            te = nc.tensor

            def three(dst, stat, mov, start, stop):
                (sh, sl), (mh, ml) = stat, mov
                te.matmul(dst, sl, mh, start=start, stop=False)
                te.matmul(dst, sh, ml, start=False, stop=False)
                return te.matmul(dst, sh, mh, start=False, stop=stop)

            def halves(hi, lo, *at):
                return hi[at], lo[at]

            pe.wait_ge(mod_in, 16)
            pe.wait_ge(silu_c_done, 1)
            for m in range(6):
                last = te.matmul(bank[6][:, m * B:(m + 1) * B], wmod[:, m * D:(m + 1) * D], silu_c[:], start=True, stop=True)
            last.then_inc(mod_mm, 1)
            pe.wait_ge(rep_done, 1)
            for b in range(B):
                last = te.matmul(bank[7][:, b * D:(b + 1) * D], silu_rep[:, b], wmod[:, GA * D:(GA + 1) * D],
                                 start=True, stop=True)
            last.then_inc(ga_mm, 1)
            pe.wait_ge(filt_in, 48)
            pe.wait_ge(mod_done, 1)
            te.matmul(bank[6][0:HID, :], w1a[:], pos_t[:], start=True, stop=True).then_inc(z_mm, 1)
            pe.wait_ge(proj_in, 64)

            def turn_norm(b, norm):
                late = norm and b >= HB
                pe.wait_ge(xhat_done, norm * B + b + 1)
                if not norm and b >= 2:
                    pe.wait_ge(h_t_done, b - 1)
                if late and b > HB:
                    pe.wait_ge(logits_copied, b - HB)
                for j in range(NJ):
                    last = te.transpose(bank[7 if late else b % 2][:, j * P:(j + 1) * P], xhat[:, b * NJ + j], ident[:])
                last.then_inc(xhat_t, 1)

            def project(m):
                g, b = conv_place(m)
                if m < B:
                    pe.wait_ge(h_t_done, b + 1)
                elif m == B:
                    pe.wait_ge(folded_done, 2)
                te.matmul(conv_bank(m)[:], w_in_t[:, g * D:(g + 1) * D], h_t[:, b], start=True,
                          stop=True).then_inc(proj_mm, 1)

            def forward(even, odd_bank, kt, moving):
                for par, dst, done in ((1, odd_bank, odd_mm), (0, even, even_mm)):
                    for part in range(2):
                        for j in range(NK):
                            last = three(dst[:, part * HW:(part + 1) * HW],
                                         halves(fwd_hi, fwd_lo, slice(None), par, j, part, slice(kt * P, (kt + 1) * P)),
                                         moving(par * NK + j), j == 0, j == NK - 1)
                    last.then_inc(done, 1)

            for b in range(B):
                turn_norm(b, 0)
            for m in range(2):
                project(m)
            pe.wait_ge(wave_done, 1)
            pe.wait_ge(zero_done, 1)
            pe.wait_ge(ga_copied, 1)
            for j in range(NJ):
                last = te.matmul(bank[6 + j // 2][:, (j % 2) * 256:(j % 2 + 1) * 256], wave[:, j * P:(j + 1) * P], w2a[:],
                                 start=True, stop=True)
                if j % 2:
                    last.then_inc(h_mm, 1)
            for m in range(2, B):
                project(m)
            pe.wait_ge(h_lo_done, 1)
            pe.wait_ge(dft_in, 32)

            def filter_forward(kt):
                forward(bank[FILTER_EVEN[kt]], bank[FILTER_ODD[kt]], kt, lambda t: (h_hi[:, t], h_lo[:, t]))

            def to_tokens(s):
                for b in step_batches(s):
                    pe.wait_ge(v_done, HB * s + b % HB + 1)
                    if s:
                        pe.wait_ge(tok_lo_done, HB * s + b % HB - 1)
                    if s == 2:
                        pe.wait_ge(gates_done, 2 + b % HB + 1)
                    for j in range(NJ):
                        par, jj = divmod(j, NK)
                        last = te.transpose(bank[b % 2][:, j * P:(j + 1) * P],
                                            v[:, b, 2 * P * jj + par:2 * P * (jj + 1):2], ident[:])
                    last.then_inc(v_t, 1)

            def step_forward(s):
                b = step_batches(s)[0]
                pe.wait_ge(tok_lo_done, HB * (s + 1))
                for kt in range(NK):
                    if s:
                        pe.wait_ge(folded_done, 2 * (NK * s + kt) + 2)
                    elif kt:
                        pe.wait_ge(folded_done, 2 * NK)
                    else:
                        pe.wait_ge(v_done, B)
                    forward(bank[STEP_EVEN[kt]], bank[STEP_ODD[kt]], kt, lambda t: (tok_hi[:, t, b:b + HB], tok_lo[:, t, b:b + HB]))

            def back(s, b):
                i = b % HB
                if s == 0:
                    pe.wait_ge(gates_done, i + 1)
                elif s < STEPS - 1:
                    pe.wait_ge(gates_done, 2 * (s + 1) + i + 1)
                if s:
                    pe.wait_ge(v_done, B + HB * (s - 1) + i + 1)
                for par in range(2):
                    for kt in range(NK):
                        pe.wait_ge(y_lo_done, 2 * (NK * s + kt) + par + 1)
                        for part in range(2):
                            at = slice(part * HW + i * D, part * HW + (i + 1) * D)
                            last = three(bank[6 + i][:, par * LH:(par + 1) * LH],
                                         halves(y_hi, y_lo, slice(None), slot(s, kt), par, at),
                                         halves(inv_hi, inv_lo, slice(None), par, kt, part),
                                         kt + part == 0, kt + part == NK)
                    if par == 0 and (s, b) == (STEPS - 1, HB):
                        turn_norm(0, 1)
                last.then_inc(inv_mm, 1)

            def attention_out(b):
                pe.wait_ge(v_done, (ORDER * B) + b + 1)
                pe.wait_ge(ga_done, b + 1)
                if b >= 2:
                    pe.wait_ge(x1_done, b - 1)
                for j in range(NJ):
                    last = te.matmul(bank[2 + b % 2][:, j * D:(j + 1) * D], v[:, b, j * P:(j + 1) * P], w_out_g[:, b],
                                     start=True, stop=True)
                last.then_inc(attn_mm, 1)

            def logits(b):
                pe.wait_ge(h2_done, b + 1)
                if b == 1:
                    pe.wait_ge(scores_done, b)
                for j in range(NJ):
                    dst = bank[4][:, (b * NJ + j) * E:(b * NJ + j + 1) * E] if b < HB else bank[7][:, j * E:(j + 1) * E]
                    last = te.matmul(dst, h2[:, b, j * P:(j + 1) * P], gate_w_t[:], start=True, stop=True)
                last.then_inc(logits_mm, 1)

            def weights_by_expert(b):
                pe.wait_ge(comb_done, b + 1)
                if b == 1:
                    pe.wait_ge(logits_copied, B - HB)
                if b >= 2:
                    pe.wait_ge(comb_t_done, b)
                    pe.wait_ge(out_done, 1)
                for j in range(NJ):
                    last = te.transpose(bank[7 if b else 5][0:E, j * P:(j + 1) * P], comb[:, b * NJ + j], ident[:])
                last.then_inc(comb_tr, 1)

            filter_forward(0)
            to_tokens(0)
            filter_forward(1)
            step_forward(0)
            to_tokens(1)
            for m in step_projections(0):
                project(m)
            for s in range(1, STEPS):
                if s >= 2:
                    to_tokens(s)
                    for m in step_projections(s):
                        project(m)
                step_forward(s)
                if s == 1:
                    for m in step_projections(1):
                        project(m)
                if s == 1:
                    pe.wait_ge(inv_in, 32)
                if s:
                    for b in step_batches(s - 1):
                        back(s - 1, b)
            for b in range(HB):
                attention_out(b)
            back(STEPS - 1, HB)
            pe.wait_ge(late_in, 16)
            logits(0)
            back(STEPS - 1, HB + 1)
            turn_norm(1, 1)
            attention_out(HB)
            logits(1)
            weights_by_expert(0)
            attention_out(B - 1)
            pe.wait_ge(h2_lo_done, 1)

            def down(b, d):
                u = d % NU
                if u == 0 and (not isinstance(b, int) or b > 0):
                    pe.wait_ge(moe_done, b)
                pe.wait_ge(act_lo_done, unit(b, d))
                three(bank[6][:], halves(w_hi, w_lo, slice(None), u, 2), (act_hi[:, half_slot(u)], act_lo[:, half_slot(u)]),
                      u == 0, u == NU - 1).then_inc(down_mm, 1)

            def turn_sum(b):
                pe.wait_ge(moe_done, b)
                if isinstance(b, int) and b == 1:
                    pe.wait_ge(comb_t_done, 2)
                for j in range(NJ):
                    last = te.transpose(bank[7][:, j * P:(j + 1) * P], moe_t[:, j * P:(j + 1) * P], ident[:])
                last.then_inc(moe_tr, 1)

            def experts(b, first):
                tokens = (h2_hi[:, bass.ds(b, 1)].rearrange("p o l -> p (o l)"),
                          h2_lo[:, bass.ds(b, 1)].rearrange("p o l -> p (o l)"))
                for u in range(NU):
                    if not first or u >= USLOTS:
                        pe.wait_ge(act_done, unit(b, before(u)))
                    if first and u == USLOTS - 1:
                        pe.wait_ge(scores_done, HB)
                        pe.wait_ge(comb_t_done, 1)
                    if first:
                        pe.wait_ge(w_lo_done, u // CHUNK + 1)
                    three(bank[GATE_BANKS[u % USLOTS]][:], halves(w_hi, w_lo, slice(None), u, 0), tokens, True, True).then_inc(gate_mm, 1)
                    if first and u < B - HB:
                        pe.wait_ge(x1_done, HB + u + 1)
                    three(bank[UP_BANKS[u % USLOTS]][:], halves(w_hi, w_lo, slice(None), u, 1), tokens, True, True).then_inc(up_mm, 1)
                    if not first or u >= LAG:
                        down(b, u - LAG)
                    if u == LAG + 1 and not first:
                        turn_sum(b)
                    if isinstance(b, int):
                        if (b, u) in TURNED_AT:
                            turn_norm(HB + TURNED_AT.index((b, u)), 1)
                        if (b, u) in LOGITS_AT:
                            logits(HB + LOGITS_AT.index((b, u)))
                        if (b, u) in WEIGHTS_TURNED_AT:
                            weights_by_expert(1 + WEIGHTS_TURNED_AT.index((b, u)))

            experts(0, True)
            pe.wait_ge(comb_t_done, 2)
            pe.wait_ge(h2_lo_done, 2)
            experts(1, False)
            pe.wait_ge(comb_t_done, B)
            pe.wait_ge(h2_lo_done, B)
            with pe.Fori(2, B) as b:
                experts(b, False)
            for d in range(-LAG, 0):
                down(B, d)
            turn_sum(B)


def kernel(**inputs):
    import numpy as _np
    import concourse.bacc as _bacc
    from concourse import mybir as _mybir
    from concourse.bass_utils import run_bass_kernel_spmd as _run

    g = {k.replace("L0_", ""): _np.asarray(a) for k, a in inputs.items()}
    f = _np.float32
    t = (_np.arange(L, dtype=f) / f(L - 1)).astype(f)
    pos = _np.sin(((t[:, None] * _np.arange(EMB, dtype=f)[None]) * f(FREQ)).astype(_np.float64))
    half = lambda a: _np.ldexp(_np.round(_np.ldexp(_np.frexp(a)[0], 12)), _np.frexp(a)[1] - 12)
    token = (_np.arange(L).reshape(LH, 2).T).ravel()
    k = _np.arange(LH)
    angle = _np.pi * ((2 * k[:, None] + 1) * (2 * token[None] + 1) % (8 * L)) / (4 * L)
    dft = _np.stack([_np.cos(angle), _np.sin(angle)])
    fwd = dft.reshape(2, LH, 2, NK, P).transpose(4, 2, 3, 0, 1)
    inv = dft.reshape(2, NK, P, 2, LH).transpose(2, 3, 1, 0, 4)
    near = k.reshape(NK, P)
    freq = _np.stack([near, L - 1 - near], 1).reshape(2 * NK, P).T
    phi = _np.pi * (2 * freq + 1) / (4 * L)
    consts = _np.concatenate([-t[token].reshape(NJ, P).T] + [a / L ** 2 for a in (_np.cos(phi), _np.sin(phi), -_np.sin(phi))], 1)
    by_group = lambda a: a.reshape(GROUPS, D).T
    cols = _np.concatenate([by_group(g["attn_b_in"])] + [by_group(g["attn_conv_w"][:, i]) for i in range(3)]
                           + [by_group(g["attn_conv_b"])], 1)
    gu = g["ffn_experts_gate_up"].reshape(PAIRS, 2, 2, INTER, D).transpose(4, 0, 2, 1, 3).reshape(D, PAIRS, 2, D)
    dn = g["ffn_experts_down"].reshape(PAIRS, 2, D, INTER).transpose(1, 3, 0, 2).reshape(D, PAIRS, 1, D)
    shared = _np.stack([g["ffn_shared_gate_w"].T, g["ffn_shared_up_w"].T, g["ffn_shared_down_w"].T], 1)
    arrays = {
        "x": g["attn_u"], "c_t": g["c"].T, "wmod": g["wmod"],
        "w1a": _np.concatenate([g["attn_w1"].T, g["attn_b1"][None]]),
        "pos_t": _np.concatenate([pos[token].T.astype(f), _np.ones((1, L), f)]),
        "w2a": _np.concatenate([g["attn_w2"].T, g["attn_b2"][None]]),
        "ident": _np.eye(P, dtype=f), "w_in_t": g["attn_w_in"].T, "cols": cols,
        "rows": _np.concatenate([g["attn_filt_decay"].ravel(), g["attn_filt_bias"].ravel(), g["attn_b_out"],
                                 g["ffn_e_score_correction_bias"]]),
        "consts": consts.astype(f), "fwd_hi": half(fwd).astype(f), "fwd_lo": half(fwd - half(fwd)).astype(f),
        "inv_hi": half(inv).astype(f), "inv_lo": half(inv - half(inv)).astype(f), "w_out_t": g["attn_w_out"].T,
        "gate_w_t": g["ffn_gate_weight"].T,
        "w_experts": _np.concatenate([_np.concatenate([gu, dn], 2), shared[:, None]], 1),
    }
    nc = _bacc.Bacc("TRN2", target_bir_lowering=False, num_devices=1)
    args, feed = {}, {}
    for name, a in arrays.items():
        feed[f"in_{name}"] = _np.ascontiguousarray(a)
        args[name] = nc.dram_tensor(f"in_{name}", a.shape, _mybir.dt.from_np(a.dtype), kind="ExternalInput").ap()
    out = nc.dram_tensor("out_0", (B, L, D), _mybir.dt.float32, kind="ExternalOutput").ap()
    build(nc, args, out)
    r = _run(nc, [feed], core_ids=[0])
    return r.results[0]["out_0"]
```
